# Optimizing a Trainium2 kernel written in Bass

```python
import numpy as np
import jax
import jax.numpy as jnp

def _softmax(x, axis=-1):
    return jax.nn.softmax(x, axis=axis)

def _gelu(x):
    return jax.nn.gelu(x, approximate=True)

def _silu(x):
    return jax.nn.silu(x)

def _sigmoid(x):
    return jax.nn.sigmoid(x)

def _layernorm(x, axis=-1, eps=1e-05):
    m = jnp.mean(x, axis=axis, keepdims=True)
    v = jnp.var(x, axis=axis, keepdims=True)
    return (x - m) / jnp.sqrt(v + eps)

def _scatter_add(tgt, idx, src, axis=0):
    return tgt.at[idx].add(src)

def _segment_sum(src, seg, n):
    return jax.ops.segment_sum(src, seg, n)
kernel_name = 'mk_adaln_ffn_d1_seqx_r4_70ee34'

def setup_inputs(seed: int=0):
    np.random.seed(seed)
    _w = jnp.asarray

    def _rec_inputs():
        import jax
        import jax.numpy as jnp
        _rk = jax.random.key(seed)
        x = -0.000125 + 0.9999 * jax.random.normal(jax.random.fold_in(_rk, 1), (64, 64, 512), jnp.float32)
        _lenS = 64 - jax.random.randint(jax.random.fold_in(_rk, 7), (64,), 0, max(1, 64 // 4) + 1, jnp.int32)
        _lenS2 = 64 - jax.random.randint(jax.random.fold_in(_rk, 8), (64,), 0, max(1, 64 // 4) + 1, jnp.int32)
        itok_B_0_7 = jax.random.randint(jax.random.fold_in(_rk, 11), (64,), 0, 8, jnp.int32)
        fside_8xS_0 = -0.00162727 + 0.0609077 * jax.random.normal(jax.random.fold_in(_rk, 12), (8, 64), jnp.float32)
        return (x, itok_B_0_7, fside_8xS_0)
    x, itok_B_0_7, fside_8xS_0 = _rec_inputs()

    def _L0_cond_setup():
        import jax, jax.numpy as jnp
        import numpy as np
        B, C, T = (64, 64, 512)
        D, N = (64, 8)
        key = jax.random.key(seed)
        k_x, k_s, k_w, k_b = jax.random.split(key, 4)
        scale = 1.0 / np.sqrt(C)
        x = jax.random.normal(k_x, (B, C, T), dtype=jnp.float32)
        subjects = jax.random.randint(k_s, (B,), 0, N, dtype=jnp.int64)
        weights = jax.random.normal(k_w, (N, C, D), dtype=jnp.float32) * scale
        bias = jax.random.normal(k_b, (N, D), dtype=jnp.float32) * scale
        return {'x': x, 'subjects': subjects, 'weights': weights, 'bias': bias}
    _L0_cond_all = _L0_cond_setup()
    _L0_cond_in = {k: v for k, v in _L0_cond_all.items() if k in ('weights',)}
    del _L0_cond_all

    def _L0_ffn_setup():
        import jax, jax.numpy as jnp
        import numpy as np
        NUM_EXPERTS = 16
        TOP_K = 4
        N_GROUP = 4
        TOPK_GROUP = 2
        SCALING = 2.5

        def _route(x, gate_weight, expert_bias):
            logits = x @ gate_weight.T
            scores = jax.nn.sigmoid(logits)
            biased = scores + expert_bias[None, :]
            T = x.shape[0]
            gsz = NUM_EXPERTS // N_GROUP
            grp = biased.reshape(T, N_GROUP, gsz)
            top2, _ = jax.lax.top_k(grp, 2)
            group_scores = top2.sum(-1)
            _, gidx = jax.lax.top_k(group_scores, TOPK_GROUP)
            gmask = jax.nn.one_hot(gidx, N_GROUP, dtype=scores.dtype).sum(1)
            emask = jnp.repeat(gmask, gsz, axis=1)
            masked = jnp.where(emask > 0, biased, -jnp.inf)
            _, sel = jax.lax.top_k(masked, TOP_K)
            w = jnp.take_along_axis(scores, sel, axis=1)
            w = w / (w.sum(-1, keepdims=True) + 1e-20)
            return (w * SCALING, sel)

        def _moe(x, w, sel, gate_proj, up_proj, down_proj):
            cw = (jax.nn.one_hot(sel, NUM_EXPERTS, dtype=x.dtype) * w[..., None]).sum(1)

            def body(acc, inp):
                g, u, d, we = inp
                y = jax.nn.silu(x @ g.T) * (x @ u.T) @ d.T
                return (acc + we[:, None] * y, None)
            out, _ = jax.lax.scan(body, jnp.zeros_like(x), (gate_proj, up_proj, down_proj, cw.T))
            return out
        key = jax.random.key(seed)
        ks = jax.random.split(key, 9)
        B, S, H, I = (2, 256, 512, 256)
        w = lambda k, shape: jax.random.normal(k, shape, jnp.float32) * 0.02
        return {'hidden_states': jax.random.normal(ks[0], (B, S, H), jnp.float32), 'gate_weight': w(ks[1], (NUM_EXPERTS, H)), 'expert_bias': jnp.zeros((NUM_EXPERTS,), jnp.float32), 'gate_proj': w(ks[2], (NUM_EXPERTS, I, H)), 'up_proj': w(ks[3], (NUM_EXPERTS, I, H)), 'down_proj': w(ks[4], (NUM_EXPERTS, H, I)), 'shared_gate': w(ks[5], (I, H)), 'shared_up': w(ks[6], (I, H)), 'shared_down': w(ks[7], (H, I))}
    _L0_ffn_all = _L0_ffn_setup()
    _L0_ffn_in = {k: v for k, v in _L0_ffn_all.items() if k in ('gate_weight', 'expert_bias', 'gate_proj', 'up_proj', 'down_proj', 'shared_gate', 'shared_up', 'shared_down')}
    del _L0_ffn_all
    return {'x': x, 'itok_B_0_7': itok_B_0_7, 'fside_8xS_0': fside_8xS_0, 'L0_cond_weights': _L0_cond_in['weights'], 'L0_ffn_gate_weight': _L0_ffn_in['gate_weight'], 'L0_ffn_expert_bias': _L0_ffn_in['expert_bias'], 'L0_ffn_gate_proj': _L0_ffn_in['gate_proj'], 'L0_ffn_up_proj': _L0_ffn_in['up_proj'], 'L0_ffn_down_proj': _L0_ffn_in['down_proj'], 'L0_ffn_shared_gate': _L0_ffn_in['shared_gate'], 'L0_ffn_shared_up': _L0_ffn_in['shared_up'], 'L0_ffn_shared_down': _L0_ffn_in['shared_down']}

def reference(x, itok_B_0_7, fside_8xS_0, L0_cond_weights, L0_ffn_gate_weight, L0_ffn_expert_bias, L0_ffn_gate_proj, L0_ffn_up_proj, L0_ffn_down_proj, L0_ffn_shared_gate, L0_ffn_shared_up, L0_ffn_shared_down):
    import jax
    import jax.numpy as jnp

    def _L0_cond_ref(x, subjects, weights, bias):
        import jax, jax.numpy as jnp
        import numpy as np
        B, C, T = (64, 64, 512)
        D, N = (64, 8)
        w = weights[subjects]
        b = bias[subjects]
        out = jnp.einsum('bct,bcd->bdt', x, w)
        out = out + b[:, :, None]
        return out

    def _L0_ffn_ref(hidden_states, gate_weight, expert_bias, gate_proj, up_proj, down_proj, shared_gate, shared_up, shared_down):
        import jax, jax.numpy as jnp
        import numpy as np
        NUM_EXPERTS = 16
        TOP_K = 4
        N_GROUP = 4
        TOPK_GROUP = 2
        SCALING = 2.5

        def _route(x, gate_weight, expert_bias):
            logits = x @ gate_weight.T
            scores = jax.nn.sigmoid(logits)
            biased = scores + expert_bias[None, :]
            T = x.shape[0]
            gsz = NUM_EXPERTS // N_GROUP
            grp = biased.reshape(T, N_GROUP, gsz)
            top2, _ = jax.lax.top_k(grp, 2)
            group_scores = top2.sum(-1)
            _, gidx = jax.lax.top_k(group_scores, TOPK_GROUP)
            gmask = jax.nn.one_hot(gidx, N_GROUP, dtype=scores.dtype).sum(1)
            emask = jnp.repeat(gmask, gsz, axis=1)
            masked = jnp.where(emask > 0, biased, -jnp.inf)
            _, sel = jax.lax.top_k(masked, TOP_K)
            w = jnp.take_along_axis(scores, sel, axis=1)
            w = w / (w.sum(-1, keepdims=True) + 1e-20)
            return (w * SCALING, sel)

        def _moe(x, w, sel, gate_proj, up_proj, down_proj):
            cw = (jax.nn.one_hot(sel, NUM_EXPERTS, dtype=x.dtype) * w[..., None]).sum(1)

            def body(acc, inp):
                g, u, d, we = inp
                y = jax.nn.silu(x @ g.T) * (x @ u.T) @ d.T
                return (acc + we[:, None] * y, None)
            out, _ = jax.lax.scan(body, jnp.zeros_like(x), (gate_proj, up_proj, down_proj, cw.T))
            return out
        B, S, H = hidden_states.shape
        x = hidden_states.reshape(-1, H)
        w, sel = _route(x, gate_weight, expert_bias)
        out = _moe(x, w, sel, gate_proj, up_proj, down_proj)
        shared = jax.nn.silu(x @ shared_gate.T) * (x @ shared_up.T) @ shared_down.T
        return (out + shared).reshape(B, S, H)
    x = x + _L0_ffn_ref(_L0_cond_ref(x, itok_B_0_7, L0_cond_weights, fside_8xS_0), L0_ffn_gate_weight, L0_ffn_expert_bias, L0_ffn_gate_proj, L0_ffn_up_proj, L0_ffn_down_proj, L0_ffn_shared_gate, L0_ffn_shared_up, L0_ffn_shared_down)
    return x

_drawn_inputs = setup_inputs


def setup_inputs(seed=0):
    import zlib

    import numpy as np

    out = dict(_drawn_inputs(seed))
    spreads = {'L0_ffn_expert_bias': (0.0, 0.1)}
    factors = {'fside_8xS_0': 6.835}
    for name, (base, spread) in spreads.items():
        noise = np.random.default_rng([zlib.crc32(name.encode()), seed]).standard_normal(out[name].shape)
        drawn = base * np.exp(spread * noise) if base else spread * noise
        out[name] = jnp.asarray(drawn.astype(out[name].dtype))
    for name, factor in factors.items():
        out[name] = (out[name] * factor).astype(out[name].dtype)
    return out
```

```python
from contextlib import ExitStack

import concourse.bass as bass
from concourse import mybir

F32 = mybir.dt.float32
I32 = mybir.dt.int32
U32 = mybir.dt.uint32
ALU = mybir.AluOpType
ACT = mybir.ActivationFunctionType
AX = mybir.AxisListType

P = 128
B, C, H = 64, 64, 512
N = B * C
NT = N // P
E, TOPK = 16, 4
NG, GS, TOPG = 4, 4, 2
SCALING = 2.5
I = 256
HK, IK = H // P, I // P
UP = HK * 2 * I
EW = UP + IK * H
NS = 8
NR = (N * TOPK + E * (P - 1)) // P
RING = 4
BIG = 3.0e38


class Tile:

    def __init__(self, rnd, slot):
        self.rnd, self.slot = rnd, slot

    def __add__(self, d):
        return Tile(self.rnd + (self.slot + d) // RING, (self.slot + d) % RING)

    def done(self, d=0):
        return self.rnd * RING + (self.slot + d)


def tile_at(n):
    return Tile(n // RING, n % RING)


def run_tiles(eng, first, head, rounds, tail, step):
    for n in range(first, first + head):
        step(tile_at(n), n)
    start = first + head
    with eng.Fori(0, rounds) as turn:
        for j in range(RING):
            step(Tile(turn + (start + j) // RING, (start + j) % RING), None)
    for n in range(start + RING * rounds, start + RING * rounds + tail):
        step(tile_at(n), n)


def build(nc, x, itok, fside, cond_w, gate_w, expert_bias, ffn_w, out):
    x_rows = x.rearrange("b c t -> (b c) t")
    h_rows = nc.dram_tensor("h_rows", [N + P, H], F32).ap()

    with ExitStack() as ctx:
        def sb(name, shape, dt=F32):
            return ctx.enter_context(nc.sbuf_tensor(name, shape, dt))

        def ps(name):
            return ctx.enter_context(nc.psum_tensor(name, [P, 512], F32))

        def sem(name):
            return ctx.enter_context(nc.semaphore(name))

        ident = sb("ident", [P, P])
        before = sb("before", [P, P])
        ones = sb("ones", [P, P])
        key16 = sb("key16", [P, E])
        iota_lane = sb("iota_lane", [P, P])
        iota_tile = sb("iota_tile", [P, NR])
        iota_full = sb("iota_full", [P, NT])
        token1 = sb("token1", [P, NT])
        pad_row = sb("pad_row", [P, 1])
        part_no = sb("part_no", [P, 1])
        zeros = sb("zeros", [P, H])
        itok_row = sb("itok_row", [1, B], I32)
        itok8 = sb("itok8", [NS, B], I32)
        subj1h = sb("subj1h", [NS, B])
        fside2 = sb("fside2", [NS, 2 * C])
        bias_tok = sb("bias_tok", [P, NT])
        gate_sb = sb("gate_sb", [P, HK * E])
        ebias = sb("ebias", [P, E])
        w_shared = sb("w_shared", [P, EW])
        w_ring = sb("w_ring", [P, 2 * EW])
        x_ring = sb("x_ring", [P, RING, H])
        cw_ring = sb("cw_ring", [P, RING, P])
        tok_ring = sb("tok_ring", [P, RING, H])
        xT = sb("xT", [P, 2, H])
        silu = sb("silu", [P, 2, I])
        hid = sb("hid", [P, 2, I])
        hidT = sb("hidT", [P, 2, I])
        y_ring = sb("y_ring", [P, RING, H])
        gidx = sb("gidx", [P, RING], U32)
        sidx = sb("sidx", [P, RING], U32)
        gidx_s = [sb(f"gidx{s}", [P, 1], U32) for s in range(RING)]
        sidx_s = [sb(f"sidx{s}", [P, 1], U32) for s in range(RING)]
        scores = sb("scores", [P, NT * E])
        biased = sb("biased", [P, NT * E])
        chosen = [sb(f"chosen{k}", [P, NT * E]) for k in range(TOPK)]
        t0 = sb("t0", [P, NT * E])
        t1 = sb("t1", [P, NT * E])
        mask = sb("mask", [P, NT * E])
        small = [sb(f"small{k}", [P, NT * NG]) for k in range(6)]
        red = sb("red", [P, NT])
        red2 = sb("red2", [P, NT])
        wk = sb("wk", [P, NT, TOPK])
        slot_f = sb("slot_f", [P, NT, TOPK])
        slot_i = sb("slot_i", [P, NT * TOPK], I32)
        part_i = sb("part_i", [P, NT * TOPK], I32)
        slot_tile = sb("slot_tile", [P, NT, TOPK])
        slot_lane = sb("slot_lane", [P, NT, TOPK])
        e0 = sb("e0", [P, E])
        e1 = sb("e1", [P, E])
        tiles_e = sb("tiles_e", [P, E])
        end_i = sb("end_i", [P, E], I32)
        cmp_te = sb("cmp_te", [1, NR * E])
        eid_f = sb("eid_f", [1, NR])
        eid = sb("eid", [1, NR], I32)
        woff = sb("woff", [1, NR], I32)
        weven = sb("weven", [1, NR], I32)
        wodd = sb("wodd", [1, NR], I32)
        lane1h = sb("lane1h", [P, 2, TOPK, P])
        tile1h = sb("tile1h", [P, TOPK, NR])
        entry = sb("entry", [P, 2, TOPK, 2, NR])
        idx_all = sb("idx_all", [P, NR], U32)
        w_slot = sb("w_slot", [P, NR])
        pad_tmp = sb("pad_tmp", [P, NR])

        psT = [ps(f"psT{i}") for i in range(2)]
        psGU = [ps(f"psGU{i}") for i in range(2)]
        psY = [ps(f"psY{i}") for i in range(2)]
        psH = ps("psH")
        psM = ps("psM")

        consts = sem("consts")
        pool_step = sem("pool_step")
        small_loaded = sem("small_loaded")
        shared_loaded = sem("shared_loaded")
        cond_in = [sem(f"cond_in{s}") for s in range(RING)]
        subj_ready = sem("subj_ready")
        bias_ps = sem("bias_ps")
        cond_done = sem("cond_done")
        h_ready = sem("h_ready")
        h_stored = [sem(f"h_stored{s}") for s in range(RING)]
        pads_stored = sem("pads_stored")
        a_xposed = sem("a_xposed")
        a_xT_ready = sem("a_xT_ready")
        logits_done = sem("logits_done")
        scored = sem("scored")
        dve = sem("dve")
        mask_ready = sem("mask_ready")
        prefix_done = sem("prefix_done")
        expert_tab = sem("expert_tab")
        entry_ready = sem("entry_ready")
        table_done = sem("table_done")
        slots_ready = sem("slots_ready")
        w_loaded = [sem(f"w_loaded{i}") for i in range(2)]
        h_loaded = [sem(f"h_loaded{s}") for s in range(RING)]
        x_loaded = [sem(f"x_loaded{s}") for s in range(RING)]
        gathered = [sem(f"gathered{s}") for s in range(RING)]
        out_stored = [sem(f"out_stored{s}") for s in range(RING)]
        scattered = sem("scattered")
        idx_copied = sem("idx_copied")
        indirect_clear = sem("indirect_clear")
        xposed = sem("xposed")
        xT_ready = sem("xT_ready")
        gu_done = sem("gu_done")
        silu_ready = sem("silu_ready")
        hid_ready = sem("hid_ready")
        hid_xposed = sem("hid_xposed")
        hidT_ready = sem("hidT_ready")
        down_done = sem("down_done")
        y_ready = sem("y_ready")

        SMALL = 6 * 16

        COND = (0, RING, NT // RING - 1, 2)
        SHARED = (0, RING, NT // RING - 2, RING)
        TURNS = (NR - 4) // RING
        ROUTED = (NT, NR - 3 - RING * TURNS, TURNS, 3)
        LAST = NT + NR - 1

        def rows(t, ap):
            return ap[bass.ds(t.done() * P, P), :]

        block = ctx.enter_context(nc.Block())

        @block.sync
        def _(sp):
            sp.dma_start(itok_row[:], itok.unsqueeze(0)).then_inc(small_loaded, 16)
            sp.dma_start(itok8[:], itok.partition_broadcast(NS)).then_inc(small_loaded, 16)
            for half in range(2):
                sp.dma_start(fside2[:, half * C:(half + 1) * C], fside).then_inc(small_loaded, 16)
            sp.dma_start(gate_sb[:], gate_w).then_inc(small_loaded, 16)
            sp.dma_start(ebias[:], expert_bias.partition_broadcast(P)).then_inc(small_loaded, 16)
            sp.wait_ge(small_loaded, SMALL)
            sp.wait_ge(consts, 1)

            def load_cond(t, n):
                if n is None or n >= RING:
                    sp.wait_ge(cond_done, t.done(1 - RING))
                sp.dma_start(x_ring[:, t.slot, :], rows(t, x_rows)).then_inc(cond_in[t.slot], 16)
                for half in range(2):
                    subject = sp.value_load(itok_row[0:1, bass.ds(t.done() * 2 + half, 1)],
                                            min_val=0, max_val=NS - 1)
                    a, b = half * C, half * C + C
                    sp.dma_start(cw_ring[a:b, t.slot, a:b],
                                 cond_w[bass.ds(subject, 1), :, :].rearrange("o c d -> (o c) d")
                                 ).then_inc(cond_in[t.slot], 16)

            run_tiles(sp, COND[0], COND[1], COND[2], 0, load_cond)
            sp.dma_start(w_shared[:], ffn_w[E]).then_inc(shared_loaded, 16)
            for e in range(2):
                sp.dma_start(w_ring[:, e * EW:(e + 1) * EW], ffn_w[e]).then_inc(w_loaded[e], 16)

            for s in range(RING):
                sp.wait_ge(h_stored[s], 16 * (NT // RING))

            def load_h(t):
                sp.dma_start(tok_ring[:, t.slot, :], rows(t, h_rows)).then_inc(h_loaded[t.slot], 16)

            def load_x(t):
                sp.dma_start(x_ring[:, t.slot, :], rows(t, x_rows)).then_inc(x_loaded[t.slot], 16)

            sp.wait_ge(a_xposed, NT)
            sp.wait_ge(cond_done, NT)
            for n in range(RING - 1):
                load_h(tile_at(n))
                load_x(tile_at(n))

            def shared_step(t, n):
                if n is None or n + 3 < NT:
                    if n is None or n > 0:
                        sp.wait_ge(xposed, t.done())
                    load_h(t + 3)
                    if n is None or n > 0:
                        sp.wait_ge(y_ready, t.done())
                    load_x(t + 3)
                sp.wait_ge(y_ready, t.done(1))
                sp.dma_start(rows(t, out), y_ring[:, t.slot, :]).then_inc(out_stored[t.slot], 16)

            run_tiles(sp, *SHARED, shared_step)

            sp.wait_ge(expert_tab, 1)
            with sp.Fori(0, E // 2 - 1) as pair:
                for j in range(2):
                    end = sp.value_load(end_i[0:1, bass.ds(pair * 2 + j, 1)], min_val=0, max_val=NR)
                    sp.wait_ge(down_done, end + NT)
                    sp.dma_start(w_ring[:, j * EW:(j + 1) * EW],
                                 ffn_w[bass.ds(pair * 2 + (j + 2), 1), :, :].rearrange("o p w -> (o p) w")
                                 ).then_inc(w_loaded[j], 16)

        @block.gpsimd
        def _(pool):
            count = [0]

            def link(ins):
                count[0] += 1
                ins.then_inc(pool_step, 1)
                pool.wait_ge(pool_step, count[0])

            pool.memset(cw_ring[:], 0.0).then_inc(consts, 1)
            link(pool.memset(zeros[:], 0.0))
            link(pool.memset(ident[:], 0.0))
            link(pool.memset(ones[:], 1.0))
            link(pool.affine_select(out=ident[:], in_=ident[:], compare_op=ALU.not_equal, fill=1.0,
                                    base=0, pattern=[[-1, P]], channel_multiplier=1))
            link(pool.affine_select(out=before[:], in_=ones[:], compare_op=ALU.is_gt, fill=0.0,
                                    base=0, pattern=[[1, P]], channel_multiplier=-1))

            def iota(t, step, base, per_partition):
                link(pool.iota(t[:], [[step, t.shape[1]]], base=base, channel_multiplier=per_partition,
                               allow_small_or_imprecise_dtypes=True))

            iota(key16, -1, E, 0)
            iota(iota_lane, 1, 0, 0)
            iota(iota_tile, 1, 0, 0)
            iota(iota_full, P, 0, 0)
            iota(token1, P, 1, 1)
            iota(pad_row, 0, N + 1, 1)
            iota(part_no, 0, 0, 1)
            pool.memset(gidx[:], 0).then_inc(consts, 1)
            pool.dma_start(h_rows[N:N + P, :], zeros[:]).then_inc(pads_stored, 16)
            pool.dma_start(out[N:N + P, :], zeros[:]).then_inc(pads_stored, 16)

            def store_h(t, n):
                pool.wait_ge(h_ready, t.done(1))
                pool.dma_start(rows(t, h_rows), tok_ring[:, t.slot, :]).then_inc(h_stored[t.slot], 16)

            run_tiles(pool, COND[0], COND[1], COND[2], 0, store_h)

            pool.wait_ge(slots_ready, 1)
            pool.wait_ge(pads_stored, 32)
            for s in range(RING):
                pool.wait_ge(h_stored[s], 16 * (NT // RING))
                pool.wait_ge(out_stored[s], 16 * (NT // RING))

            def copy_idx(dst, t, nth):
                pool.tensor_copy(dst[:], idx_all[:, bass.ds(t.done(-NT), 1)]).then_inc(idx_copied, 1)
                pool.wait_ge(idx_copied, nth)

            def gather(t, nth):
                copy_idx(gidx_s[t.slot], t, nth)
                pool.sem_inc(indirect_clear, 1)
                pool.indirect_dma_start(tok_ring[:, t.slot, :], None, h_rows[:, :],
                                        bass.IndirectOffsetOnAxis(gidx_s[t.slot][:], 0)
                                        ).then_inc(gathered[t.slot], 16)

            pool.wait_ge(xposed, NT)
            for n in range(3):
                gather(tile_at(NT + n), n + 1)

            def routed_step(t, n):
                r = t.done(-NT)
                if n is None or n + 3 <= LAST:
                    if n != NT:
                        pool.wait_ge(xposed, t.done())
                    gather(t + 3, r * 2 + 4)
                    nth = r * 2 + 5
                else:
                    nth = 2 * (NR - 3) + 3 + (n - (LAST - 2))  + 1
                copy_idx(sidx_s[t.slot], t, nth)
                pool.wait_ge(y_ready, t.done(1))
                if n != NT:
                    pool.wait_ge(scattered, r * 16)
                pool.sem_inc(indirect_clear, 1)
                pool.indirect_dma_start(out[:, :], bass.IndirectOffsetOnAxis(sidx_s[t.slot][:], 0),
                                        y_ring[:, t.slot, :], None, compute_op=ALU.add
                                        ).then_inc(scattered, 16)

            run_tiles(pool, *ROUTED, routed_step)
            pool.wait_ge(scattered, 16 * NR)

        @block.scalar
        def _(act):
            def cond_step(t, n):
                if n is None or 1 <= n <= NT:
                    act.wait_ge(a_xposed, t.done())
                    if n is None or n >= 3:
                        act.wait_ge(logits_done, t.done(-2))
                    act.activation(xT[:, (t.slot + 1) % 2, :], psT[(t.slot + 1) % 2][:], ACT.Copy
                                   ).then_inc(a_xT_ready, 1)
                if n is None or n >= 2:
                    act.wait_ge(logits_done, t.done(-1))
                    act.activation(scores[:, bass.ds(t.done(-2) * E, E)], psGU[t.slot % 2][:, 0:E],
                                   ACT.Sigmoid).then_inc(scored, 1)

            run_tiles(act, *COND, cond_step)

            def copy_xT(t, n):
                act.wait_ge(xposed, t.done(1))
                if n is None or n >= 2:
                    act.wait_ge(gu_done, t.done(-1))
                act.activation(xT[:, t.slot % 2, :], psT[t.slot % 2][:], ACT.Copy).then_inc(xT_ready, 1)

            def copy_hidT(t, n):
                act.wait_ge(hid_xposed, t.done(1))
                if n is None or n >= 2:
                    act.wait_ge(down_done, t.done(-1))
                act.activation(hidT[:, t.slot % 2, :], psH[:, 0:I], ACT.Copy).then_inc(hidT_ready, 1)

            def ffn(run, last):
                first = run[0]

                def step(t, n):
                    if n != first:
                        copy_hidT(t + -1, None if n is None else n - 1)
                    if n is None or n < last:
                        copy_xT(t + 1, None if n is None else n + 1)
                    act.wait_ge(gu_done, t.done(1))
                    if n is None or n >= 2:
                        act.wait_ge(hid_ready, t.done(-1))
                    act.activation(silu[:, t.slot % 2, :], psGU[t.slot % 2][:, 0:I], ACT.Silu
                                   ).then_inc(silu_ready, 1)

                copy_xT(tile_at(first), first)
                run_tiles(act, *run, step)
                copy_hidT(tile_at(last), last)

            ffn(SHARED, NT - 1)
            ffn(ROUTED, LAST)

        @block.tensor
        def _(pe):
            pe.wait_ge(consts, 2)
            pe.wait_ge(small_loaded, SMALL)
            pe.wait_ge(subj_ready, 1)
            subj = subj1h[:, :].rearrange("n (c two) -> n two c", two=2)
            for half in range(2):
                mm = pe.matmul(psH[:, half * NT:(half + 1) * NT], fside2[:], subj[:, half, :],
                               start=True, stop=True)
            mm.then_inc(bias_ps, 1)

            def transposes(dst, src, parts):
                for k in range(parts):
                    mm = pe.transpose(dst[:, k * P:(k + 1) * P], src[:, k * P:(k + 1) * P], ident[:])
                return mm

            def cond_step(t, n):
                if n is None or n < NT:
                    pe.wait_ge(cond_in[t.slot], (t.rnd + 1) * 48)
                    if n is None or n >= 2:
                        pe.wait_ge(h_ready, t.done(-1))
                    pe.matmul(psY[t.slot % 2][:], cw_ring[:, t.slot, :], x_ring[:, t.slot, :],
                              start=True, stop=True).then_inc(cond_done, 1)
                if n is None or 1 <= n <= NT:
                    u = t + -1
                    pe.wait_ge(h_ready, t.done())
                    if n is None or n >= 3:
                        pe.wait_ge(a_xT_ready, t.done(-2))
                    transposes(psT[u.slot % 2], tok_ring[:, u.slot, :], HK).then_inc(a_xposed, 1)
                if n is None or n >= 2:
                    pe.wait_ge(a_xT_ready, t.done(-1))
                    if n is None or n >= 4:
                        pe.wait_ge(scored, t.done(-3))
                    for k in range(HK):
                        mm = pe.matmul(psGU[t.slot % 2][:, 0:E], xT[:, t.slot % 2, k * P:(k + 1) * P],
                                       gate_sb[:, k * E:(k + 1) * E], start=(k == 0), stop=(k == HK - 1))
                    mm.then_inc(logits_done, 1)

            run_tiles(pe, *COND, cond_step)
            pe.wait_ge(scored, NT)
            pe.wait_ge(shared_loaded, 16)

            def xpose(t, n, routed):
                if routed:
                    pe.wait_ge(gathered[t.slot], (t.rnd - (NT // RING - 1)) * 16)
                else:
                    pe.wait_ge(h_loaded[t.slot], (t.rnd + 1) * 16)
                if n is None or n >= 2:
                    pe.wait_ge(xT_ready, t.done(-1))
                transposes(psT[t.slot % 2], tok_ring[:, t.slot, :], HK).then_inc(xposed, 1)

            def xpose_hid(t, n):
                pe.wait_ge(hid_ready, t.done(1))
                if n is None or n >= 1:
                    pe.wait_ge(hidT_ready, t.done())
                transposes(psH, hid[:, t.slot % 2, :], IK).then_inc(hid_xposed, 1)

            def weights(t, routed):
                if not routed:
                    return lambda col: w_shared[:, col:col + H]
                at = pe.value_load(woff[0:1, bass.ds(t.done(-NT), 1)], min_val=0, max_val=EW)
                return lambda col: w_ring[:, bass.ds(at + col, H)]

            def loads(t, routed):
                if not routed:
                    return ()
                return [(loaded, pe.value_load(table[0:1, bass.ds(t.done(-NT), 1)], min_val=0, max_val=16 * E))
                        for table, loaded in ((weven, w_loaded[0]), (wodd, w_loaded[1]))]

            def gate_up(t, n, w, needs):
                for loaded, needed in needs:
                    pe.wait_ge(loaded, needed)
                pe.wait_ge(xT_ready, t.done(1))
                if n is None or n >= 2:
                    pe.wait_ge(hid_ready, t.done(-1))
                for k in range(HK):
                    mm = pe.matmul(psGU[t.slot % 2][:], xT[:, t.slot % 2, k * P:(k + 1) * P],
                                   w(k * 2 * I), start=(k == 0), stop=(k == HK - 1))
                mm.then_inc(gu_done, 1)

            def down(t, n, w):
                pe.wait_ge(hidT_ready, t.done(1))
                if n is None or n >= 2:
                    pe.wait_ge(y_ready, t.done(-1))
                for k in range(IK):
                    mm = pe.matmul(psY[t.slot % 2][:], hidT[:, t.slot % 2, k * P:(k + 1) * P],
                                   w(UP + k * H), start=(k == 0), stop=(k == IK - 1))
                mm.then_inc(down_done, 1)

            def fill_slots(t, n):
                pe.wait_ge(entry_ready, t.done(1))
                for k in range(TOPK):
                    mm = pe.matmul(psM[:, 0:2 * NR], lane1h[:, t.slot % 2, k, :],
                                   entry[:, t.slot % 2, k, :, :].rearrange("p a r -> p (a r)"),
                                   start=(n == 0 and k == 0), stop=(n == NT - 1 and k == TOPK - 1),
                                   skip_group_check=True)
                mm.then_inc(table_done, 1)

            def ffn(run, last, routed):
                first = run[0]

                def step(t, n):
                    prev = None if n is None else n - 1
                    w, needs = weights(t, routed), loads(t, routed)
                    w_prev = weights(t + -1, routed) if n != first else None
                    if n != first:
                        xpose_hid(t + -1, prev)
                    if n is None or n < last:
                        xpose(t + 1, None if n is None else n + 1, routed)
                    gate_up(t, n, w, needs)
                    if n != first:
                        down(t + -1, prev, w_prev)
                        if not routed:
                            fill_slots(t + -1, prev)
                    elif not routed:
                        pe.wait_ge(mask_ready, 1)
                        pe.matmul(psH[:], before[:], mask[:], start=True, stop=True)
                        pe.matmul(psM[:], ones[:], mask[:], start=True, stop=True).then_inc(prefix_done, 1)

                xpose(tile_at(first), first, routed)
                run_tiles(pe, *run, step)
                w = weights(tile_at(last), routed)
                xpose_hid(tile_at(last), last)
                down(tile_at(last), last, w)
                if not routed:
                    fill_slots(tile_at(last), last)

            ffn(SHARED, NT - 1, False)
            pe.wait_ge(expert_tab, 1)
            ffn(ROUTED, LAST, True)

        @block.vector
        def _(v):
            count = [0]

            def link(ins):
                count[0] += 1
                ins.then_inc(dve, 1)
                v.wait_ge(dve, count[0])

            def tt(o, a, b, op):
                link(v.tensor_tensor(o, a, b, op))

            v.wait_ge(consts, 2)
            v.wait_ge(small_loaded, SMALL)
            v.tensor_scalar(subj1h[:], itok8[:], part_no[0:NS, 0:1], None, ALU.is_equal).then_inc(subj_ready, 1)
            v.wait_ge(bias_ps, 1)
            for half in range(2):
                a, b = half * C, half * C + C
                link(v.tensor_copy(bias_tok[a:b, :], psH[a:b, half * NT:(half + 1) * NT]))

            def cond_step(t, n):
                v.wait_ge(cond_done, t.done(1))
                if n is None or n >= RING:
                    v.wait_ge(h_stored[t.slot], t.rnd * 16)
                    v.wait_ge(a_xposed, t.done(1 - RING))
                v.tensor_scalar(tok_ring[:, t.slot, :], psY[t.slot % 2][:], bias_tok[:, bass.ds(t.done(), 1)],
                                None, ALU.add).then_inc(h_ready, 1)

            run_tiles(v, COND[0], COND[1], COND[2], 0, cond_step)

            def per_chunk(ap, n):
                return ap.rearrange("p (c n) -> p c n", n=n)

            def spread(ap, n):
                return ap.unsqueeze(2).to_broadcast([P, ap.shape[1], n])

            def over_chunks(ap):
                return ap.unsqueeze(1).to_broadcast([P, NT, ap.shape[1]])

            def pick(onehot, values, n, keys, again):
                val, one, tmp = per_chunk(values, n), per_chunk(onehot, n), per_chunk(t1[:, 0:NT * n], n)
                link(v.tensor_reduce(red[:], val, AX.X, ALU.max))
                tt(tmp, val, spread(red[:], n), ALU.is_equal)
                tt(tmp, tmp, over_chunks(keys), ALU.mult)
                link(v.tensor_reduce(red2[:], tmp, AX.X, ALU.max))
                tt(one, tmp, spread(red2[:], n), ALU.is_equal)
                if again:
                    link(v.scalar_tensor_tensor(out=values, in0=onehot, scalar=-BIG, in1=values,
                                                op0=ALU.mult, op1=ALU.add))

            v.wait_ge(scored, NT)
            tt(per_chunk(biased[:], E), per_chunk(scores[:], E), over_chunks(ebias[:]), ALU.add)
            four = biased[:, :].rearrange("p (g j) -> p j g", j=GS)
            hi1, lo1, hi2, lo2, s4, s5 = [s[:] for s in small]
            tt(hi1, four[:, 0, :], four[:, 1, :], ALU.max)
            tt(lo1, four[:, 0, :], four[:, 1, :], ALU.min)
            tt(hi2, four[:, 2, :], four[:, 3, :], ALU.max)
            tt(lo2, four[:, 2, :], four[:, 3, :], ALU.min)
            tt(s4, hi1, hi2, ALU.max)
            tt(s5, hi1, hi2, ALU.min)
            tt(lo1, lo1, lo2, ALU.max)
            tt(s5, s5, lo1, ALU.max)
            tt(s4, s4, s5, ALU.add)
            pick(hi1, s4, NG, key16[:, E - NG:E], True)
            pick(hi2, s4, NG, key16[:, E - NG:E], False)
            tt(hi1, hi1, hi2, ALU.add)
            link(v.tensor_scalar(hi1, hi1, -1.0, BIG, ALU.add, ALU.mult))
            by_group = biased[:, :].rearrange("p (g j) -> p g j", j=GS)
            tt(by_group, by_group, spread(hi1, GS), ALU.add)
            for k in range(TOPK):
                pick(chosen[k][:], biased[:], E, key16[:], k < TOPK - 1)
            tt(mask[:], chosen[0][:], chosen[1][:], ALU.add)
            tt(t0[:], chosen[2][:], chosen[3][:], ALU.add)
            v.tensor_tensor(mask[:], mask[:], t0[:], ALU.add).then_inc(mask_ready, 1)
            v.wait_ge(mask_ready, 1)

            for k in range(TOPK):
                tt(t0[:], chosen[k][:], scores[:], ALU.mult)
                link(v.tensor_reduce(wk[:, :, k], per_chunk(t0[:], E), AX.X, ALU.add))
            link(v.tensor_reduce(red[:], wk[:], AX.X, ALU.add))
            link(v.tensor_scalar(red[:], red[:], 1e-20, None, ALU.add))
            link(v.reciprocal(red[:], red[:]))
            tt(wk[:], wk[:], spread(red[:], TOPK), ALU.mult)
            link(v.tensor_scalar(wk[:], wk[:], SCALING, None, ALU.mult))

            v.wait_ge(prefix_done, 1)
            link(v.tensor_copy(t0[:], psM[:]))
            src, dst = t0, t1
            d = 1
            while d < NT:
                v.tensor_copy(dst[:, 0:d * E], src[:, 0:d * E])
                tt(dst[:, d * E:], src[:, d * E:], src[:, 0:(NT - d) * E], ALU.add)
                src, dst = dst, src
                d *= 2
            total = src[:, (NT - 1) * E:NT * E]
            steps = biased[:, :].rearrange("p (e j) -> p e j", j=NT)
            tt(steps, spread(total, NT), iota_full[:].unsqueeze(1).to_broadcast([P, E, NT]), ALU.is_gt)
            link(v.tensor_reduce(tiles_e[:], steps, AX.X, ALU.add))
            es, ed = tiles_e, e0
            d = 1
            while d < E:
                v.tensor_copy(ed[:, 0:d], es[:, 0:d])
                tt(ed[:, d:], es[:, d:], es[:, 0:E - d], ALU.add)
                es, ed = ed, (e1 if ed is e0 else e0)
                d *= 2
            ends = es
            link(v.tensor_copy(end_i[:], ends[:]))
            starts = e0 if ends is e1 else e1
            tt(starts[:], ends[:], tiles_e[:], ALU.subtract)
            link(v.tensor_scalar(starts[:], starts[:], float(P), None, ALU.mult))
            link(v.tensor_tensor(dst[:], src[:], psM[:], ALU.subtract))
            tt(dst[:], dst[:], psH[:], ALU.add)
            tt(per_chunk(dst[:], E), per_chunk(dst[:], E), over_chunks(starts[:]), ALU.add)
            for k in range(TOPK):
                tt(src[:], chosen[k][:], dst[:], ALU.mult)
                link(v.tensor_reduce(slot_f[:, :, k], per_chunk(src[:], E), AX.X, ALU.add))
            link(v.tensor_copy(slot_i[:], slot_f[:].rearrange("p c k -> p (c k)")))
            link(v.tensor_scalar(part_i[:], slot_i[:], P.bit_length() - 1, None, ALU.logical_shift_right))
            link(v.tensor_copy(slot_tile[:].rearrange("p c k -> p (c k)"), part_i[:]))
            link(v.tensor_scalar(part_i[:], slot_i[:], P - 1, None, ALU.bitwise_and))
            link(v.tensor_copy(slot_lane[:].rearrange("p c k -> p (c k)"), part_i[:]))
            te = cmp_te[:, :].rearrange("p (r e) -> p r e", e=E)
            tt(te, iota_tile[0:1, :].unsqueeze(2).to_broadcast([1, NR, E]),
               ends[0:1, :].unsqueeze(1).to_broadcast([1, NR, E]), ALU.is_ge)
            link(v.tensor_reduce(eid_f[:], te, AX.X, ALU.add))
            link(v.tensor_scalar(eid[:], eid_f[:], float(E - 1), None, ALU.min))
            link(v.tensor_scalar(woff[:], eid[:], 1, None, ALU.bitwise_and))
            link(v.tensor_scalar(woff[:], woff[:], float(EW), None, ALU.mult))
            link(v.tensor_scalar(weven[:], eid[:], 1, None, ALU.logical_shift_right))
            link(v.tensor_scalar(weven[:], weven[:], 16.0, 16.0, ALU.mult, ALU.add))
            link(v.tensor_scalar(wodd[:], eid[:], 1.0, None, ALU.add))
            link(v.tensor_scalar(wodd[:], wodd[:], 1, None, ALU.logical_shift_right))
            v.tensor_scalar(wodd[:], wodd[:], 1.0, 16.0, ALU.max, ALU.mult).then_inc(expert_tab, 1)

            def mix(t, n):
                v.wait_ge(silu_ready, t.done(1))
                if n is None or n >= 2:
                    v.wait_ge(hid_xposed, t.done(-1))
                v.tensor_tensor(hid[:, t.slot % 2, :], silu[:, t.slot % 2, :], psGU[t.slot % 2][:, I:2 * I],
                                ALU.mult).then_inc(hid_ready, 1)

            def finish(t, n, routed):
                v.wait_ge(down_done, t.done(1))
                if routed:
                    if n is None or n >= NT + RING:
                        v.wait_ge(scattered, t.done(1 - RING - NT) * 16)
                    elif n >= NT:
                        v.wait_ge(out_stored[t.slot], 16 * (NT // RING))
                    v.tensor_scalar(y_ring[:, t.slot, :], psY[t.slot % 2][:],
                                    w_slot[:, bass.ds(t.done(-NT), 1)], None, ALU.mult).then_inc(y_ready, 1)
                else:
                    if n is None or n >= RING:
                        v.wait_ge(out_stored[t.slot], t.rnd * 16)
                    v.wait_ge(x_loaded[t.slot], (t.rnd + 1) * 16)
                    v.tensor_tensor(y_ring[:, t.slot, :], psY[t.slot % 2][:], x_ring[:, t.slot, :],
                                    ALU.add).then_inc(y_ready, 1)

            base = count[0]

            def make_entries(t, n):
                c = t.done()
                if n is None or n >= 2:
                    v.wait_ge(table_done, t.done(-1))
                lanes = slot_lane[:, bass.ds(c, 1), :].rearrange("p o k -> p (o k)")
                tiles = slot_tile[:, bass.ds(c, 1), :].rearrange("p o k -> p (o k)")
                wts = wk[:, bass.ds(c, 1), :].rearrange("p o k -> p (o k)")
                v.tensor_tensor(lane1h[:, t.slot % 2], iota_lane[:].unsqueeze(1).to_broadcast([P, TOPK, P]),
                                lanes.unsqueeze(2).to_broadcast([P, TOPK, P]), ALU.is_equal)
                if n is None or n >= 1:
                    v.wait_ge(entry_ready, t.done())
                v.tensor_tensor(tile1h[:], iota_tile[:].unsqueeze(1).to_broadcast([P, TOPK, NR]),
                                tiles.unsqueeze(2).to_broadcast([P, TOPK, NR]), ALU.is_equal).then_inc(dve, 1)
                v.wait_ge(dve, t.done(1) + base)
                v.tensor_scalar(entry[:, t.slot % 2, :, 0, :], tile1h[:], token1[:, bass.ds(c, 1)], None, ALU.mult)
                v.tensor_tensor(entry[:, t.slot % 2, :, 1, :], tile1h[:],
                                wts.unsqueeze(2).to_broadcast([P, TOPK, NR]), ALU.mult).then_inc(entry_ready, 1)

            def ffn(run, last, routed):
                first = run[0]

                def step(t, n):
                    mix(t, n)
                    if n != first:
                        finish(t + -1, None if n is None else n - 1, routed)
                    if not routed:
                        make_entries(t, n)

                run_tiles(v, *run, step)
                finish(tile_at(last), last, routed)

            ffn(SHARED, NT - 1, False)
            v.wait_ge(table_done, NT)
            count[0] += NT
            link(v.tensor_scalar(pad_tmp[:], psM[:, 0:NR], 0.0, pad_row[:, 0:1], ALU.is_equal, ALU.mult))
            link(v.scalar_tensor_tensor(out=idx_all[:], in0=psM[:, 0:NR], scalar=-1.0, in1=pad_tmp[:],
                                        op0=ALU.add, op1=ALU.add))
            link(v.tensor_copy(w_slot[:], psM[:, NR:2 * NR]))
            v.sem_inc(slots_ready, 1)
            ffn(ROUTED, LAST, True)


def kernel(x, itok_B_0_7, fside_8xS_0, L0_cond_weights, L0_ffn_gate_weight, L0_ffn_expert_bias,
           L0_ffn_gate_proj, L0_ffn_up_proj, L0_ffn_down_proj, L0_ffn_shared_gate, L0_ffn_shared_up,
           L0_ffn_shared_down):
    import numpy as np
    import concourse.bacc as bacc
    from concourse.bass_utils import run_bass_kernel_spmd as run

    def columns(w):
        e, n, k = w.shape
        return w.transpose(0, 2, 1).reshape(e, k // P, P, n).transpose(0, 2, 1, 3)

    gate = np.concatenate([L0_ffn_gate_proj, np.asarray(L0_ffn_shared_gate)[None]])
    up = np.concatenate([L0_ffn_up_proj, np.asarray(L0_ffn_shared_up)[None]])
    down = np.concatenate([L0_ffn_down_proj, np.asarray(L0_ffn_shared_down)[None]])
    ffn_w = np.concatenate([np.concatenate([columns(gate), columns(up)], axis=3).reshape(E + 1, P, UP),
                            columns(down).reshape(E + 1, P, IK * H)], axis=2)
    arrays = {
        "x": np.ascontiguousarray(x),
        "itok": np.ascontiguousarray(itok_B_0_7),
        "fside": np.ascontiguousarray(fside_8xS_0),
        "cond_w": np.ascontiguousarray(L0_cond_weights),
        "gate_w": np.ascontiguousarray(columns(np.asarray(L0_ffn_gate_weight)[None])[0].reshape(P, HK * E)),
        "expert_bias": np.ascontiguousarray(L0_ffn_expert_bias),
        "ffn_w": np.ascontiguousarray(ffn_w),
    }
    nc = bacc.Bacc("TRN2", target_bir_lowering=False, num_devices=1)
    args = [nc.dram_tensor(n, a.shape, mybir.dt.from_np(a.dtype), kind="ExternalInput").ap()
            for n, a in arrays.items()]
    out = nc.dram_tensor("out", [N + P, H], F32, kind="ExternalOutput").ap()
    build(nc, *args, out)
    r = run(nc, [arrays], core_ids=[0])
    return r.results[0]["out"][:N].reshape(B, C, H)
```

```python
from contextlib import ExitStack

import concourse.bass as bass
from concourse import mybir

F32 = mybir.dt.float32
F32R = mybir.dt.float32r
I32 = mybir.dt.int32
U32 = mybir.dt.uint32
ALU = mybir.AluOpType
ACT = mybir.ActivationFunctionType
AX = mybir.AxisListType

P = 128
B, C, H = 64, 64, 512
N = B * C
NT = N // P
E, TOPK = 16, 4
NG, GS, TOPG = 4, 4, 2
SCALING = 2.5
I = 256
HK, IK = H // P, I // P
UP = HK * 2 * I
EW = UP + IK * H
NS = 8
NR = (N * TOPK + E * (P - 1)) // P
NRP = NR + NR % 2
RING = 4
BIG = 3.0e38


class Tile:

    def __init__(self, rnd, slot):
        self.rnd, self.slot = rnd, slot

    def __add__(self, d):
        return Tile(self.rnd + (self.slot + d) // RING, (self.slot + d) % RING)

    def done(self, d=0):
        return self.rnd * RING + (self.slot + d)


def tile_at(n):
    return Tile(n // RING, n % RING)


def run_tiles(eng, first, head, rounds, tail, step):
    for n in range(first, first + head):
        step(tile_at(n), n)
    start = first + head
    with eng.Fori(0, rounds) as turn:
        for j in range(RING):
            step(Tile(turn + (start + j) // RING, (start + j) % RING), None)
    for n in range(start + RING * rounds, start + RING * rounds + tail):
        step(tile_at(n), n)


def build(nc, x, itok, fside, cond_w, gate_w, expert_bias, ffn_w, out):
    x_rows = x.rearrange("b c t -> (b c) t")
    h_rows = nc.dram_tensor("h_rows", [N + P, H + E], F32).ap()

    with ExitStack() as ctx:
        def sb(name, shape, dt=F32):
            return ctx.enter_context(nc.sbuf_tensor(name, shape, dt))

        def ps(name):
            return ctx.enter_context(nc.psum_tensor(name, [P, 512], F32))

        def sem(name):
            return ctx.enter_context(nc.semaphore(name))

        ident = sb("ident", [P, P])
        before = sb("before", [P, P])
        ones = sb("ones", [P, P])
        key16 = sb("key16", [P, E])
        iota_lane = sb("iota_lane", [P, P])
        iota_tile = sb("iota_tile", [P, NRP])
        iota_full = sb("iota_full", [P, NT])
        token1 = sb("token1", [P, NT])
        pad_row = sb("pad_row", [P, 1])
        part_no = sb("part_no", [P, 1])
        itok_row = sb("itok_row", [1, B], I32)
        itok8 = sb("itok8", [NS, B], I32)
        subj1h = sb("subj1h", [NS, B])
        fside2 = sb("fside2", [NS, 2 * C])
        bias_tok = sb("bias_tok", [P, NT])
        gate_sb = sb("gate_sb", [P, HK * E])
        ebias = sb("ebias", [P, E])
        raw_w = sb("raw_w", [P, 2 * EW])
        split_w = sb("split_w", [P, 2 * 2 * EW], F32R)
        cond_sb = sb("cond_sb", [P, NS * C])
        x_all = sb("x_all", [P, NT, H])
        cw_ring = sb("cw_ring", [P, RING, P])
        tok_ring = sb("tok_ring", [P, RING, H + E])
        aT = sb("aT", [P, 2, H])
        xT_hi = sb("xT_hi", [P, 2, H], F32R)
        xT_lo = sb("xT_lo", [P, 2, H], F32R)
        silu, hid = aT[:, :, 0:I], aT[:, :, I:2 * I]
        hidT_hi = sb("hidT_hi", [P, 2, I], F32R)
        hidT_lo = sb("hidT_lo", [P, 2, I], F32R)
        y_ring = sb("y_ring", [P, RING, H])
        zeros = y_ring[:].rearrange("p r h -> p (r h)")[:, 0:H + E]
        gidx_s = [sb(f"gidx{s}", [P, 1], U32) for s in range(RING)]
        sidx_s = [sb(f"sidx{s}", [P, 1], U32) for s in range(RING)]
        scores = sb("scores", [P, NT * E])
        passing = [raw_w[:, EW + k * NT * E:EW + (k + 1) * NT * E] for k in range(TOPK + 2)]
        assert (TOPK + 2) * NT * E <= EW and (NR + E + 2) * E <= EW
        biased, t0, chosen = passing[0], passing[1], passing[2:]
        t1 = sb("t1", [P, NT * E])
        mask = sb("mask", [P, NT * E])
        small = [aT[:, k % 2, k // 2 * NT * NG:(k // 2 + 1) * NT * NG] for k in range(6)]
        red = sb("red", [P, NT])
        red2 = sb("red2", [P, NT])
        weights_te = sb("weights_te", [P, NT, E])
        slot_f = sb("slot_f", [P, NT, TOPK])
        slot_i = sb("slot_i", [P, NT * TOPK], I32)
        part_i = sb("part_i", [P, NT * TOPK], I32)
        slot_tile = sb("slot_tile", [P, NT, TOPK])
        slot_lane = sb("slot_lane", [P, NT, TOPK])
        e0 = sb("e0", [P, E])
        e1 = sb("e1", [P, E])
        tiles_e = sb("tiles_e", [P, E])
        used = sb("used", [1, E])
        turn_e = sb("turn_e", [1, E])
        turn_tmp = sb("turn_tmp", [1, E])
        n_used = sb("n_used", [1, 1])
        cmp_te = raw_w[0:1, EW:EW + NR * E]
        cmp_qe = raw_w[0:1, EW + NR * E:EW + (NR + E + 2) * E]
        order_f = sb("order_f", [1, E + 2])
        eid_f = sb("eid_f", [1, NR])
        turn_f = sb("turn_f", [1, NR + 1])
        prep_f = sb("prep_f", [1, NR])
        prep_t = sb("prep_t", [1, NR])
        order = sb("order", [1, E + 2], I32)
        eid = sb("eid", [1, NR], I32)
        turn_i = sb("turn_i", [1, NR + 1], I32)
        woff = sb("woff", [1, NR], I32)
        need = sb("need", [1, NR], I32)
        prep_odd = sb("prep_odd", [1, NR], I32)
        prep = sb("prep", [1, NR], I32)
        lane1h = sb("lane1h", [P, 2, TOPK, P], F32R)
        entry = sb("entry", [P, 2, TOPK, NRP], F32R)
        idx_all = sb("idx_all", [P, NR], U32)
        pad_tmp = sb("pad_tmp", [P, NR])

        psT = [ps(f"psT{i}") for i in range(2)]
        psGU = [ps(f"psGU{i}") for i in range(2)]
        psY = [ps(f"psY{i}") for i in range(2)]
        psH = ps("psH")
        psM = ps("psM")

        consts = sem("consts")
        pool_step = sem("pool_step")
        small_loaded = sem("small_loaded")
        raw_loaded = sem("raw_loaded")
        shared_loaded = sem("shared_loaded")
        high_ready = sem("high_ready")
        split_done = sem("split_done")
        x_in = [sem(f"x_in{s}") for s in range(RING)]
        cond_w_ready = sem("cond_w_ready")
        weights_ready = sem("weights_ready")
        weights_stored = sem("weights_stored")
        xhi_ready = sem("xhi_ready")
        hidhi_ready = sem("hidhi_ready")
        subj_ready = sem("subj_ready")
        bias_ps = sem("bias_ps")
        cond_done = sem("cond_done")
        h_ready = sem("h_ready")
        h_stored = [sem(f"h_stored{s}") for s in range(RING)]
        pads_stored = sem("pads_stored")
        a_xposed = sem("a_xposed")
        a_xT_ready = sem("a_xT_ready")
        logits_done = sem("logits_done")
        scored = sem("scored")
        dve = sem("dve")
        mask_ready = sem("mask_ready")
        prefix_done = sem("prefix_done")
        expert_tab = sem("expert_tab")
        entry_ready = sem("entry_ready")
        table_done = sem("table_done")
        slots_ready = sem("slots_ready")
        h_loaded = [sem(f"h_loaded{s}") for s in range(RING)]
        gathered = [sem(f"gathered{s}") for s in range(RING)]
        out_stored = [sem(f"out_stored{s}") for s in range(RING)]
        scattered = sem("scattered")
        idx_copied = sem("idx_copied")
        pool_clear = sem("pool_clear")
        xposed = sem("xposed")
        xT_ready = sem("xT_ready")
        gu_done = sem("gu_done")
        silu_ready = sem("silu_ready")
        hid_ready = sem("hid_ready")
        hid_xposed = sem("hid_xposed")
        hidT_ready = sem("hidT_ready")
        down_done = sem("down_done")
        y_ready = sem("y_ready")

        SMALL = 8 * 16

        COND = (0, RING, NT // RING - 1, 2)
        SHARED = (0, RING, NT // RING - 2, RING)
        TURNS = (NR - 4) // RING
        ROUTED = (NT, NR - 3 - RING * TURNS, TURNS, 3)
        LAST = NT + NR - 1

        def split_slot(parity):
            return (raw_w[:, bass.ds(parity * EW, EW)], split_w[:, bass.ds(parity * (2 * EW), EW)],
                    split_w[:, bass.ds(parity * (2 * EW) + EW, EW)])

        def rows(t, ap):
            return ap[bass.ds(t.done() * P, P), 0:H]

        block = ctx.enter_context(nc.Block())

        @block.sync
        def _(sp):
            sp.dma_start(itok_row[:], itok.unsqueeze(0)).then_inc(small_loaded, 16)
            sp.dma_start(itok8[:], itok.partition_broadcast(NS)).then_inc(small_loaded, 16)
            for half in range(2):
                sp.dma_start(fside2[:, half * C:(half + 1) * C], fside).then_inc(small_loaded, 16)
                sp.dma_start(cond_sb[half * C:(half + 1) * C, :].rearrange("c (n d) -> c n d", d=C),
                             cond_w.rearrange("n c d -> c n d")).then_inc(small_loaded, 16)
            sp.dma_start(gate_sb[:], gate_w).then_inc(small_loaded, 16)
            sp.dma_start(ebias[:], expert_bias.partition_broadcast(P)).then_inc(small_loaded, 16)

            def load_x(t, n):
                if n is None or n >= RING:
                    sp.wait_ge(x_in[t.slot], t.rnd * 16)
                sp.dma_start(x_all[:, bass.ds(t.done(), 1), :].rearrange("p o h -> p (o h)"),
                             rows(t, x_rows)).then_inc(x_in[t.slot], 16)

            for n in range(RING):
                load_x(tile_at(n), n)

            def cond_step(t, n):
                if n is None or n + RING < NT:
                    load_x(t + RING, None if n is None else n + RING)
                elif n + RING == NT:
                    sp.dma_start(raw_w[:, 0:EW], ffn_w[E]).then_inc(shared_loaded, 16)
                sp.wait_ge(h_ready, t.done(1))
                sp.dma_start(rows(t, h_rows), tok_ring[:, t.slot, 0:H]).then_inc(h_stored[t.slot], 16)

            run_tiles(sp, 0, RING, NT // RING - 2, RING, cond_step)

            for s in range(RING):
                sp.wait_ge(h_stored[s], 16 * (NT // RING))

            def load_h(t):
                sp.dma_start(tok_ring[:, t.slot, 0:H], rows(t, h_rows)).then_inc(h_loaded[t.slot], 16)

            sp.wait_ge(a_xposed, NT)
            for n in range(RING - 1):
                load_h(tile_at(n))

            def shared_step(t, n):
                if n is None or n + 3 < NT:
                    if n is None or n > 0:
                        sp.wait_ge(xposed, t.done())
                    load_h(t + 3)
                sp.wait_ge(y_ready, t.done(1))
                sp.dma_start(rows(t, out), y_ring[:, t.slot, :]).then_inc(out_stored[t.slot], 16)

            run_tiles(sp, *SHARED, shared_step)

        @block.gpsimd
        def _(pool):
            count = [0]

            def link(ins):
                count[0] += 1
                ins.then_inc(pool_step, 1)
                pool.wait_ge(pool_step, count[0])

            link(pool.memset(cw_ring[:], 0.0))
            link(pool.memset(zeros, 0.0))
            link(pool.memset(ident[:], 0.0))
            link(pool.memset(ones[:], 1.0))
            link(pool.affine_select(out=ident[:], in_=ident[:], compare_op=ALU.not_equal, fill=1.0,
                                    base=0, pattern=[[-1, P]], channel_multiplier=1))
            link(pool.affine_select(out=before[:], in_=ones[:], compare_op=ALU.is_gt, fill=0.0,
                                    base=0, pattern=[[1, P]], channel_multiplier=-1))

            def iota(t, step, base, per_partition):
                link(pool.iota(t[:], [[step, t.shape[1]]], base=base, channel_multiplier=per_partition,
                               allow_small_or_imprecise_dtypes=True))

            iota(key16, -1, E, 0)
            iota(iota_lane, 1, 0, 0)
            iota(iota_tile, 1, 0, 0)
            iota(iota_full, P, 0, 0)
            iota(token1, P, 1, 1)
            iota(pad_row, 0, N + 1, 1)
            iota(part_no, 0, 0, 1)
            pool.sem_inc(consts, 1)
            pool.dma_start(h_rows[N:N + P, :], zeros).then_inc(pads_stored, 16)
            pool.dma_start(out[N:N + P, :], zeros[:, 0:H]).then_inc(pads_stored, 16)

            pool.wait_ge(small_loaded, SMALL)

            def cond_step(t, n):
                for half in range(2):
                    subject = pool.value_load(itok_row[0:1, bass.ds(t.done() * 2 + half, 1)],
                                              min_val=0, max_val=NS - 1)
                    if half == 0 and (n is None or n >= RING):
                        pool.wait_ge(cond_done, t.done(1 - RING))
                        pool.sem_inc(pool_clear, 1)
                    a, b = half * C, half * C + C
                    pool.tensor_copy(cw_ring[a:b, t.slot, a:b],
                                     cond_sb[a:b, bass.ds(subject * C, C)]).then_inc(cond_w_ready, 1)

            run_tiles(pool, COND[0], COND[1], COND[2], 0, cond_step)

            def split_low(parity, turn):
                raw, high, low = split_slot(parity)
                pool.wait_ge(high_ready, turn + 1)
                pool.sem_inc(pool_clear, 1)
                pool.tensor_tensor(low, raw, high.bitcast(F32), ALU.subtract).then_inc(split_done, 1)

            def load_raw(turn, turn_mod):
                expert = pool.value_load(order[0:1, bass.ds(turn, 1)], min_val=0, max_val=E - 1)
                pool.dma_start(raw_w[:, bass.ds(turn_mod * EW, EW)],
                               ffn_w[bass.ds(expert, 1), :, :].rearrange("o p w -> (o p) w")
                               ).then_inc(raw_loaded, 16)

            pool.wait_ge(cond_w_ready, 2 * NT)
            split_low(0, 0)
            pool.wait_ge(expert_tab, 1)
            load_raw(1, 1)
            split_low(1, 1)
            pool.wait_ge(raw_loaded, 16)
            pool.wait_ge(split_done, 1)
            load_raw(2, 0)
            pool.wait_ge(weights_ready, 1)
            pool.dma_start(h_rows[0:N, H:H + E].rearrange("(c p) e -> p c e", p=P), weights_te[:]
                           ).then_inc(weights_stored, 16)

            pool.wait_ge(weights_stored, 16)
            pool.wait_ge(slots_ready, 1)
            pool.wait_ge(pads_stored, 32)
            for s in range(RING):
                pool.wait_ge(h_stored[s], 16 * (NT // RING))
                pool.wait_ge(out_stored[s], 16 * (NT // RING))

            def copy_idx(dst, t, nth):
                pool.tensor_copy(dst[:], idx_all[:, bass.ds(t.done(-NT), 1)]).then_inc(idx_copied, 1)
                pool.wait_ge(idx_copied, nth)

            def gather(t, nth):
                copy_idx(gidx_s[t.slot], t, nth)
                pool.sem_inc(pool_clear, 1)
                pool.indirect_dma_start(tok_ring[:, t.slot, :], None, h_rows[:, :],
                                        bass.IndirectOffsetOnAxis(gidx_s[t.slot][:], 0)
                                        ).then_inc(gathered[t.slot], 16)

            def scatter(t, n, nth):
                copy_idx(sidx_s[t.slot], t, nth)
                pool.wait_ge(y_ready, t.done(1))
                if n != NT:
                    pool.wait_ge(scattered, t.done(-NT) * 16)
                pool.sem_inc(pool_clear, 1)
                pool.indirect_dma_start(out[:, :], bass.IndirectOffsetOnAxis(sidx_s[t.slot][:], 0),
                                        y_ring[:, t.slot, :], None, compute_op=ALU.add
                                        ).then_inc(scattered, 16)

            pool.wait_ge(xposed, NT)
            for n in range(3):
                gather(tile_at(NT + n), n + 1)

            def routed_step(t, n):
                r = t.done(-NT)
                if n is None or n + 3 <= LAST:
                    if n != NT:
                        pool.wait_ge(hid_ready, t.done())
                    gather(t + 3, r * 2 + (4 if n == NT else 3))
                    nth = r * 2 + 4
                else:
                    nth = 2 * (NR - 3) + 3 + (n - (LAST - 2))
                if n != NT:
                    next_weights(r + -1)
                    scatter(t + -1, None if n is None else n - 1, nth)

            def next_weights(r):
                turn = pool.value_load(prep[0:1, bass.ds(r, 1)], min_val=0, max_val=E)
                with pool.If(turn):
                    odd = pool.value_load(prep_odd[0:1, bass.ds(r, 1)], min_val=0, max_val=1)
                    split_low(odd, turn)
                    pool.wait_ge(split_done, turn + 1)
                    pool.sem_inc(pool_clear, 1)
                    load_raw(turn + 1, 1 - odd)

            run_tiles(pool, *ROUTED, routed_step)
            scatter(tile_at(LAST), LAST, 2 * NR)
            pool.wait_ge(scattered, 16 * NR)

        @block.scalar
        def _(act):
            def cond_step(t, n):
                if n is None or 1 <= n <= NT:
                    act.wait_ge(a_xposed, t.done())
                    if n is None or n >= 3:
                        act.wait_ge(logits_done, t.done(-2))
                    act.activation(aT[:, (t.slot + 1) % 2, :], psT[(t.slot + 1) % 2][:], ACT.Copy
                                   ).then_inc(a_xT_ready, 1)
                if n is None or n >= 2:
                    act.wait_ge(logits_done, t.done(-1))
                    act.activation(scores[:, bass.ds(t.done(-2) * E, E)], psGU[t.slot % 2][:, 0:E],
                                   ACT.Sigmoid).then_inc(scored, 1)

            run_tiles(act, *COND, cond_step)

            def copy_xT(t, n):
                act.wait_ge(xposed, t.done(1))
                if n is None or n >= 2:
                    act.wait_ge(gu_done, t.done(-1))
                act.activation(xT_hi[:, t.slot % 2, :], psT[t.slot % 2][:], ACT.Copy).then_inc(xhi_ready, 1)

            def copy_hidT(t, n):
                act.wait_ge(hid_xposed, t.done(1))
                if n is None or n >= 2:
                    act.wait_ge(down_done, t.done(-1))
                act.activation(hidT_hi[:, t.slot % 2, :], psH[:, 0:I], ACT.Copy).then_inc(hidhi_ready, 1)

            def split_high(parity):
                raw, high, low = split_slot(parity)
                act.activation(high, raw, ACT.Copy).then_inc(high_ready, 1)

            def next_weights(t):
                turn = act.value_load(prep[0:1, bass.ds(t.done(-NT), 1)], min_val=0, max_val=E)
                with act.If(turn):
                    odd = act.value_load(prep_odd[0:1, bass.ds(t.done(-NT), 1)], min_val=0, max_val=1)
                    act.wait_ge(raw_loaded, turn * 16)
                    act.wait_ge(down_done, t.done())
                    split_high(odd)

            def ffn(run, last, routed):
                first = run[0]

                def step(t, n):
                    if n != first:
                        copy_hidT(t + -1, None if n is None else n - 1)
                    if n is None or n < last:
                        copy_xT(t + 1, None if n is None else n + 1)
                    act.wait_ge(gu_done, t.done(1))
                    if n is None or n >= 2:
                        act.wait_ge(hid_ready, t.done(-1))
                    act.activation(silu[:, t.slot % 2, :], psGU[t.slot % 2][:, 0:I], ACT.Silu
                                   ).then_inc(silu_ready, 1)
                    if routed:
                        next_weights(t)
                    elif n == first:
                        act.wait_ge(raw_loaded, 16)
                        split_high(1)

                copy_xT(tile_at(first), first)
                run_tiles(act, *run, step)
                copy_hidT(tile_at(last), last)

            act.wait_ge(shared_loaded, 16)
            split_high(0)
            ffn(SHARED, NT - 1, False)
            act.wait_ge(expert_tab, 1)
            ffn(ROUTED, LAST, True)

        @block.tensor
        def _(pe):
            pe.wait_ge(consts, 1)
            pe.wait_ge(small_loaded, SMALL)
            pe.wait_ge(subj_ready, 1)
            subj = subj1h[:, :].rearrange("n (c two) -> n two c", two=2)
            for half in range(2):
                mm = pe.matmul(psH[:, half * NT:(half + 1) * NT], fside2[:], subj[:, half, :],
                               start=True, stop=True)
            mm.then_inc(bias_ps, 1)

            def transposes(dst, src, parts):
                for k in range(parts):
                    mm = pe.transpose(dst[:, k * P:(k + 1) * P], src[:, k * P:(k + 1) * P], ident[:])
                return mm

            def cond_step(t, n):
                if n is None or n < NT:
                    pe.wait_ge(x_in[t.slot], (t.rnd + 1) * 16)
                    pe.wait_ge(cond_w_ready, t.done(1) * 2)
                    if n is None or n >= 2:
                        pe.wait_ge(h_ready, t.done(-1))
                    pe.matmul(psY[t.slot % 2][:], cw_ring[:, t.slot, :],
                              x_all[:, bass.ds(t.done(), 1), :].rearrange("p o h -> p (o h)"),
                              start=True, stop=True).then_inc(cond_done, 1)
                if n is None or 1 <= n <= NT:
                    u = t + -1
                    pe.wait_ge(h_ready, t.done())
                    if n is None or n >= 3:
                        pe.wait_ge(a_xT_ready, t.done(-2))
                    transposes(psT[u.slot % 2], tok_ring[:, u.slot, 0:H], HK).then_inc(a_xposed, 1)
                if n is None or n >= 2:
                    pe.wait_ge(a_xT_ready, t.done(-1))
                    if n is None or n >= 4:
                        pe.wait_ge(scored, t.done(-3))
                    for k in range(HK):
                        mm = pe.matmul(psGU[t.slot % 2][:, 0:E], aT[:, t.slot % 2, k * P:(k + 1) * P],
                                       gate_sb[:, k * E:(k + 1) * E], start=(k == 0), stop=(k == HK - 1))
                    mm.then_inc(logits_done, 1)

            run_tiles(pe, *COND, cond_step)
            pe.wait_ge(scored, NT)
            pe.wait_ge(mask_ready, 1)
            pe.matmul(psH[:], before[:], mask[:], start=True, stop=True)
            pe.matmul(psM[:], ones[:], mask[:], start=True, stop=True).then_inc(prefix_done, 1)
            pe.wait_ge(split_done, 1)

            def xpose(t, n, routed):
                if routed:
                    pe.wait_ge(gathered[t.slot], (t.rnd - (NT // RING - 1)) * 16)
                else:
                    pe.wait_ge(h_loaded[t.slot], (t.rnd + 1) * 16)
                if n is None or n >= 2:
                    pe.wait_ge(xT_ready, t.done(-1))
                transposes(psT[t.slot % 2], tok_ring[:, t.slot, 0:H], HK).then_inc(xposed, 1)

            def xpose_hid(t, n):
                pe.wait_ge(hid_ready, t.done(1))
                if n is None or n >= 1:
                    pe.wait_ge(hidT_ready, t.done())
                transposes(psH, hid[:, t.slot % 2, :], IK).then_inc(hid_xposed, 1)

            def weights(t, routed):
                if not routed:
                    return lambda col: split_w[:, col:col + H]
                at = pe.value_load(woff[0:1, bass.ds(t.done(-NT), 1)], min_val=0, max_val=2 * EW)
                return lambda col: split_w[:, bass.ds(at + col, H)]

            def split_product(dst, high, low, slot, parts, w, col):
                for k in range(parts):
                    c = slice(k * P, (k + 1) * P)
                    for a, at in ((high, 0), (high, EW), (low, 0)):
                        mm = pe.matmul(dst, a[:, slot, c], w(at + col + k * H), start=(k == 0 and a is high and at == 0),
                                       stop=(k == parts - 1 and a is low))
                return mm

            def gate_up(t, n, w, needed):
                if needed is not None:
                    pe.wait_ge(split_done, needed)
                pe.wait_ge(xT_ready, t.done(1))
                if n is None or n >= 2:
                    pe.wait_ge(hid_ready, t.done(-1))
                split_product(psGU[t.slot % 2][:], xT_hi, xT_lo, t.slot % 2, HK, w, 0).then_inc(gu_done, 1)

            def down(t, n, w):
                pe.wait_ge(hidT_ready, t.done(1))
                if n is None or n >= 2:
                    pe.wait_ge(y_ready, t.done(-1))
                split_product(psY[t.slot % 2][:], hidT_hi, hidT_lo, t.slot % 2, IK, w, UP).then_inc(down_done, 1)

            def fill_slots(t, n):
                pe.wait_ge(entry_ready, t.done(1))
                for k in range(TOPK):
                    mm = pe.matmul(psM[:, 0:NRP], lane1h[:, t.slot % 2, k, :], entry[:, t.slot % 2, k, :],
                                   start=(n == 0 and k == 0), stop=(n == NT - 1 and k == TOPK - 1),
                                   skip_group_check=True)
                mm.then_inc(table_done, 1)

            def ffn(run, last, routed):
                first = run[0]

                def step(t, n):
                    prev = None if n is None else n - 1
                    w = weights(t, routed)
                    needed = None
                    if routed:
                        needed = pe.value_load(need[0:1, bass.ds(t.done(-NT), 1)], min_val=1, max_val=E + 1)
                    w_prev = weights(t + -1, routed) if n != first else None
                    if n != first:
                        xpose_hid(t + -1, prev)
                    if n is None or n < last:
                        xpose(t + 1, None if n is None else n + 1, routed)
                    gate_up(t, n, w, needed)
                    if n != first:
                        down(t + -1, prev, w_prev)
                        if not routed:
                            fill_slots(t + -1, prev)

                xpose(tile_at(first), first, routed)
                run_tiles(pe, *run, step)
                w = weights(tile_at(last), routed)
                xpose_hid(tile_at(last), last)
                down(tile_at(last), last, w)
                if not routed:
                    fill_slots(tile_at(last), last)

            ffn(SHARED, NT - 1, False)
            pe.wait_ge(expert_tab, 1)
            ffn(ROUTED, LAST, True)

        @block.vector
        def _(v):
            count = [0]

            def link(ins):
                count[0] += 1
                ins.then_inc(dve, 1)
                v.wait_ge(dve, count[0])

            def tt(o, a, b, op):
                link(v.tensor_tensor(o, a, b, op))

            v.wait_ge(consts, 1)
            v.wait_ge(small_loaded, SMALL)
            v.tensor_scalar(subj1h[:], itok8[:], part_no[0:NS, 0:1], None, ALU.is_equal).then_inc(subj_ready, 1)
            v.wait_ge(bias_ps, 1)
            for half in range(2):
                a, b = half * C, half * C + C
                link(v.tensor_copy(bias_tok[a:b, :], psH[a:b, half * NT:(half + 1) * NT]))

            def cond_step(t, n):
                v.wait_ge(cond_done, t.done(1))
                if n is None or n >= RING:
                    v.wait_ge(h_stored[t.slot], t.rnd * 16)
                    v.wait_ge(a_xposed, t.done(1 - RING))
                v.tensor_scalar(tok_ring[:, t.slot, 0:H], psY[t.slot % 2][:], bias_tok[:, bass.ds(t.done(), 1)],
                                None, ALU.add).then_inc(h_ready, 1)

            run_tiles(v, COND[0], COND[1], COND[2], 0, cond_step)

            def per_chunk(ap, n):
                return ap.rearrange("p (c n) -> p c n", n=n)

            def spread(ap, n):
                return ap.unsqueeze(2).to_broadcast([P, ap.shape[1], n])

            def over_chunks(ap):
                return ap.unsqueeze(1).to_broadcast([P, NT, ap.shape[1]])

            def pick(onehot, values, n, keys, again):
                val, one, tmp = per_chunk(values, n), per_chunk(onehot, n), per_chunk(t1[:, 0:NT * n], n)
                link(v.tensor_reduce(red[:], val, AX.X, ALU.max))
                tt(tmp, val, spread(red[:], n), ALU.is_equal)
                tt(tmp, tmp, over_chunks(keys), ALU.mult)
                link(v.tensor_reduce(red2[:], tmp, AX.X, ALU.max))
                tt(one, tmp, spread(red2[:], n), ALU.is_equal)
                if again:
                    link(v.scalar_tensor_tensor(out=values, in0=onehot, scalar=-BIG, in1=values,
                                                op0=ALU.mult, op1=ALU.add))

            v.wait_ge(scored, NT)
            tt(per_chunk(biased[:], E), per_chunk(scores[:], E), over_chunks(ebias[:]), ALU.add)
            four = biased[:, :].rearrange("p (g j) -> p j g", j=GS)
            hi1, lo1, hi2, lo2, s4, s5 = small
            tt(hi1, four[:, 0, :], four[:, 1, :], ALU.max)
            tt(lo1, four[:, 0, :], four[:, 1, :], ALU.min)
            tt(hi2, four[:, 2, :], four[:, 3, :], ALU.max)
            tt(lo2, four[:, 2, :], four[:, 3, :], ALU.min)
            tt(s4, hi1, hi2, ALU.max)
            tt(s5, hi1, hi2, ALU.min)
            tt(lo1, lo1, lo2, ALU.max)
            tt(s5, s5, lo1, ALU.max)
            tt(s4, s4, s5, ALU.add)
            pick(hi1, s4, NG, key16[:, E - NG:E], True)
            pick(hi2, s4, NG, key16[:, E - NG:E], False)
            tt(hi1, hi1, hi2, ALU.add)
            link(v.tensor_scalar(hi1, hi1, -1.0, BIG, ALU.add, ALU.mult))
            by_group = biased[:, :].rearrange("p (g j) -> p g j", j=GS)
            tt(by_group, by_group, spread(hi1, GS), ALU.add)
            for k in range(TOPK):
                pick(chosen[k][:], biased[:], E, key16[:], k < TOPK - 1)
            tt(mask[:], chosen[0][:], chosen[1][:], ALU.add)
            tt(t0[:], chosen[2][:], chosen[3][:], ALU.add)
            v.tensor_tensor(mask[:], mask[:], t0[:], ALU.add).then_inc(mask_ready, 1)
            v.wait_ge(mask_ready, 1)

            by_token = weights_te[:].rearrange("p c e -> p (c e)")
            tt(by_token, mask[:], scores[:], ALU.mult)
            link(v.tensor_reduce(red[:], weights_te[:], AX.X, ALU.add))
            link(v.tensor_scalar(red[:], red[:], 1e-20, None, ALU.add))
            link(v.reciprocal(red[:], red[:]))
            tt(weights_te[:], weights_te[:], spread(red[:], E), ALU.mult)
            v.tensor_scalar(by_token, by_token, SCALING, None, ALU.mult).then_inc(weights_ready, 1)

            v.wait_ge(prefix_done, 1)
            link(v.tensor_copy(t0[:], psM[:]))
            src, dst = t0, t1
            d = 1
            while d < NT:
                v.tensor_copy(dst[:, 0:d * E], src[:, 0:d * E])
                tt(dst[:, d * E:], src[:, d * E:], src[:, 0:(NT - d) * E], ALU.add)
                src, dst = dst, src
                d *= 2
            total = src[:, (NT - 1) * E:NT * E]
            steps = biased[:, :].rearrange("p (e j) -> p e j", j=NT)
            tt(steps, spread(total, NT), iota_full[:].unsqueeze(1).to_broadcast([P, E, NT]), ALU.is_gt)
            link(v.tensor_reduce(tiles_e[:], steps, AX.X, ALU.add))
            es, ed = tiles_e, e0
            d = 1
            while d < E:
                v.tensor_copy(ed[:, 0:d], es[:, 0:d])
                tt(ed[:, d:], es[:, d:], es[:, 0:E - d], ALU.add)
                es, ed = ed, (e1 if ed is e0 else e0)
                d *= 2
            ends = es
            starts = e0 if ends is e1 else e1
            tt(starts[:], ends[:], tiles_e[:], ALU.subtract)
            link(v.tensor_scalar(starts[:], starts[:], float(P), None, ALU.mult))
            link(v.tensor_tensor(dst[:], src[:], psM[:], ALU.subtract))
            tt(dst[:], dst[:], psH[:], ALU.add)
            tt(per_chunk(dst[:], E), per_chunk(dst[:], E), over_chunks(starts[:]), ALU.add)
            for k in range(TOPK):
                tt(src[:], chosen[k][:], dst[:], ALU.mult)
                link(v.tensor_reduce(slot_f[:, :, k], per_chunk(src[:], E), AX.X, ALU.add))
            link(v.tensor_copy(slot_i[:], slot_f[:].rearrange("p c k -> p (c k)")))
            link(v.tensor_scalar(part_i[:], slot_i[:], P.bit_length() - 1, None, ALU.logical_shift_right))
            link(v.tensor_copy(slot_tile[:].rearrange("p c k -> p (c k)"), part_i[:]))
            link(v.tensor_scalar(part_i[:], slot_i[:], P - 1, None, ALU.bitwise_and))
            link(v.tensor_copy(slot_lane[:].rearrange("p c k -> p (c k)"), part_i[:]))
            link(v.tensor_scalar(used[:], tiles_e[0:1, :], 0.0, None, ALU.is_gt))
            link(v.tensor_reduce(n_used[:], used[:], AX.X, ALU.add))
            qs, qd = used, turn_e
            d = 1
            while d < E:
                v.tensor_copy(qd[:, 0:d], qs[:, 0:d])
                tt(qd[:, d:], qs[:, d:], qs[:, 0:E - d], ALU.add)
                qs, qd = qd, (turn_tmp if qd is turn_e else turn_e)
                d *= 2
            tt(qd[:], qs[:], used[:], ALU.mult)
            expert_no = iota_tile[0:1, 0:E]
            qe = cmp_qe[:, :].rearrange("p (q e) -> p q e", e=E)
            tt(qe, iota_tile[0:1, 0:E + 2].unsqueeze(2).to_broadcast([1, E + 2, E]),
               qd[:].unsqueeze(1).to_broadcast([1, E + 2, E]), ALU.is_equal)
            tt(qe, qe, expert_no.unsqueeze(1).to_broadcast([1, E + 2, E]), ALU.mult)
            link(v.tensor_reduce(order_f[:, 1:E + 2], qe[:, 1:E + 2, :], AX.X, ALU.add))
            link(v.memset(order_f[:, 0:1], 0.0))
            link(v.tensor_copy(order[:], order_f[:]))
            te = cmp_te[:, :].rearrange("p (r e) -> p r e", e=E)
            tt(te, iota_tile[0:1, 0:NR].unsqueeze(2).to_broadcast([1, NR, E]),
               ends[0:1, :].unsqueeze(1).to_broadcast([1, NR, E]), ALU.is_ge)
            link(v.tensor_reduce(eid_f[:], te, AX.X, ALU.add))
            link(v.tensor_scalar(eid[:], eid_f[:], float(E - 1), None, ALU.min))
            tt(te, te, used[:].unsqueeze(1).to_broadcast([1, NR, E]), ALU.mult)
            link(v.memset(turn_f[:, 0:1], 0.0))
            link(v.tensor_reduce(turn_f[:, 1:NR + 1], te, AX.X, ALU.add))
            link(v.tensor_scalar(turn_f[:, 1:NR + 1], turn_f[:, 1:NR + 1], 1.0, n_used[:, 0:1], ALU.add, ALU.min))
            link(v.tensor_copy(turn_i[:], turn_f[:]))
            link(v.tensor_scalar(need[:], turn_f[:, 1:NR + 1], 1.0, None, ALU.add))
            link(v.tensor_scalar(turn_i[:], turn_i[:], 1, None, ALU.bitwise_and))
            link(v.tensor_scalar(woff[:], turn_i[:, 1:NR + 1], float(2 * EW), None, ALU.mult))
            tt(prep_t[:], turn_f[:, 1:NR + 1], turn_f[:, 0:NR], ALU.not_equal)
            link(v.tensor_scalar(prep_f[:], turn_f[:, 1:NR + 1], n_used[:, 0:1], None, ALU.is_lt))
            tt(prep_t[:], prep_t[:], prep_f[:], ALU.mult)
            link(v.tensor_scalar(prep_f[:], turn_f[:, 1:NR + 1], 1.0, None, ALU.add))
            tt(prep_t[:], prep_t[:], prep_f[:], ALU.mult)
            link(v.tensor_copy(prep[:], prep_t[:]))
            v.tensor_scalar(prep_odd[:], prep[:], 1, None, ALU.bitwise_and).then_inc(expert_tab, 1)

            def split_x(t):
                v.wait_ge(xhi_ready, t.done(1))
                v.tensor_tensor(xT_lo[:, t.slot % 2, :], psT[t.slot % 2][:], xT_hi[:, t.slot % 2, :].bitcast(F32),
                                ALU.subtract).then_inc(xT_ready, 1)

            def split_hid(t):
                v.wait_ge(hidhi_ready, t.done(1))
                v.tensor_tensor(hidT_lo[:, t.slot % 2, :], psH[:, 0:I], hidT_hi[:, t.slot % 2, :].bitcast(F32),
                                ALU.subtract).then_inc(hidT_ready, 1)

            def mix(t, n, expert):
                v.wait_ge(silu_ready, t.done(1))
                if n is None or n >= 2:
                    v.wait_ge(hid_xposed, t.done(-1))
                half = t.slot % 2
                gate, up = silu[:, half, :], psGU[half][:, I:2 * I]
                if expert is None:
                    ins = v.tensor_tensor(hid[:, half, :], gate, up, ALU.mult)
                else:
                    ins = v.scalar_tensor_tensor(out=hid[:, half, :], in0=gate,
                                                 scalar=tok_ring[:, t.slot, bass.ds(expert + H, 1)],
                                                 in1=up, op0=ALU.mult, op1=ALU.mult)
                ins.then_inc(hid_ready, 1)

            def finish(t, n, routed):
                v.wait_ge(down_done, t.done(1))
                if routed:
                    if n is None or n >= NT + RING:
                        v.wait_ge(scattered, t.done(1 - RING - NT) * 16)
                    else:
                        v.wait_ge(out_stored[t.slot], 16 * (NT // RING))
                    v.tensor_copy(y_ring[:, t.slot, :], psY[t.slot % 2][:]).then_inc(y_ready, 1)
                else:
                    if n is None or n >= RING:
                        v.wait_ge(out_stored[t.slot], t.rnd * 16)
                    elif n < 2:
                        v.wait_ge(pads_stored, 32)
                    v.tensor_tensor(y_ring[:, t.slot, :], psY[t.slot % 2][:],
                                    x_all[:, bass.ds(t.done(), 1), :].rearrange("p o h -> p (o h)"),
                                    ALU.add).then_inc(y_ready, 1)

            def make_entries(t, n):
                c = t.done()
                if n is None or n >= 2:
                    v.wait_ge(table_done, t.done(-1))
                half = t.slot % 2
                lanes = slot_lane[:, bass.ds(c, 1), :].rearrange("p o k -> p (o k)")
                v.tensor_tensor(lane1h[:, half], iota_lane[:].unsqueeze(1).to_broadcast([P, TOPK, P]),
                                lanes.unsqueeze(2).to_broadcast([P, TOPK, P]), ALU.is_equal)
                for k in range(TOPK):
                    ins = v.tensor_scalar(entry[:, half, k, :], iota_tile[:],
                                          slot_tile[:, bass.ds(c, 1), k:k + 1].rearrange("p o k -> p (o k)"),
                                          token1[:, bass.ds(c, 1)], ALU.is_equal, ALU.mult)
                ins.then_inc(entry_ready, 1)

            def ffn(run, last, routed):
                first = run[0]

                def step(t, n):
                    expert = None
                    if routed:
                        expert = v.value_load(eid[0:1, bass.ds(t.done(-NT), 1)], min_val=0, max_val=E - 1)
                    if n != first:
                        split_hid(t + -1)
                    if n is None or n < last:
                        split_x(t + 1)
                    mix(t, n, expert)
                    if n != first:
                        finish(t + -1, None if n is None else n - 1, routed)
                    if not routed:
                        make_entries(t, n)

                split_x(tile_at(first))
                run_tiles(v, *run, step)
                split_hid(tile_at(last))
                finish(tile_at(last), last, routed)

            ffn(SHARED, NT - 1, False)
            v.wait_ge(table_done, NT)
            link(v.tensor_scalar(pad_tmp[:], psM[:, 0:NR], 0.0, pad_row[:, 0:1], ALU.is_equal, ALU.mult))
            v.scalar_tensor_tensor(out=idx_all[:], in0=psM[:, 0:NR], scalar=-1.0, in1=pad_tmp[:],
                                   op0=ALU.add, op1=ALU.add).then_inc(slots_ready, 1)
            ffn(ROUTED, LAST, True)


def kernel(x, itok_B_0_7, fside_8xS_0, L0_cond_weights, L0_ffn_gate_weight, L0_ffn_expert_bias,
           L0_ffn_gate_proj, L0_ffn_up_proj, L0_ffn_down_proj, L0_ffn_shared_gate, L0_ffn_shared_up,
           L0_ffn_shared_down):
    import numpy as np
    import concourse.bacc as bacc
    from concourse.bass_utils import run_bass_kernel_spmd as run

    def columns(w):
        e, n, k = w.shape
        return w.transpose(0, 2, 1).reshape(e, k // P, P, n).transpose(0, 2, 1, 3)

    gate = np.concatenate([L0_ffn_gate_proj, np.asarray(L0_ffn_shared_gate)[None]])
    up = np.concatenate([L0_ffn_up_proj, np.asarray(L0_ffn_shared_up)[None]])
    down = np.concatenate([L0_ffn_down_proj, np.asarray(L0_ffn_shared_down)[None]])
    ffn_w = np.concatenate([np.concatenate([columns(gate), columns(up)], axis=3).reshape(E + 1, P, UP),
                            columns(down).reshape(E + 1, P, IK * H)], axis=2)
    arrays = {
        "x": np.ascontiguousarray(x),
        "itok": np.ascontiguousarray(itok_B_0_7),
        "fside": np.ascontiguousarray(fside_8xS_0),
        "cond_w": np.ascontiguousarray(L0_cond_weights),
        "gate_w": np.ascontiguousarray(columns(np.asarray(L0_ffn_gate_weight)[None])[0].reshape(P, HK * E)),
        "expert_bias": np.ascontiguousarray(L0_ffn_expert_bias),
        "ffn_w": np.ascontiguousarray(ffn_w),
    }
    nc = bacc.Bacc("TRN2", target_bir_lowering=False, num_devices=1)
    args = [nc.dram_tensor(n, a.shape, mybir.dt.from_np(a.dtype), kind="ExternalInput").ap()
            for n, a in arrays.items()]
    out = nc.dram_tensor("out", [N + P, H], F32, kind="ExternalOutput").ap()
    build(nc, *args, out)
    r = run(nc, [arrays], core_ids=[0])
    return r.results[0]["out"][:N].reshape(B, C, H)
```

```python
from contextlib import ExitStack

import concourse.bass as bass
from concourse import mybir

F32 = mybir.dt.float32
F32R = mybir.dt.float32r
I32 = mybir.dt.int32
U32 = mybir.dt.uint32
ALU = mybir.AluOpType
ACT = mybir.ActivationFunctionType
AX = mybir.AxisListType

P = 128
B, C, H = 64, 64, 512
N = B * C
NT = N // P
E, TOPK = 16, 4
NG, GS, TOPG = 4, 4, 2
SCALING = 2.5
I = 256
HK, IK = H // P, I // P
UP = HK * 2 * I
EW = UP + IK * H
BC = 8
NB = NT // BC
SPLITS = 3
NS = 8
NR = (N * TOPK + E * (P - 1)) // P
NRP = NR + NR % 2
RING = 8
AHEAD = 6
BIG = 3.0e38


class Tile:

    def __init__(self, rnd, slot):
        self.rnd, self.slot = rnd, slot

    def __add__(self, d):
        return Tile(self.rnd + (self.slot + d) // RING, (self.slot + d) % RING)

    def done(self, d=0):
        return self.rnd * RING + (self.slot + d)


def tile_at(n):
    return Tile(n // RING, n % RING)


def run_tiles(eng, first, head, rounds, tail, step):
    for n in range(first, first + head):
        step(tile_at(n), n)
    start = first + head
    unroll = 2 if rounds % 2 == 0 else 1
    with eng.Fori(0, rounds // unroll) as turn:
        for j in range(unroll * RING):
            step(Tile(turn * unroll + (start + j) // RING, (start + j) % RING), None)
    for n in range(start + RING * rounds, start + RING * rounds + tail):
        step(tile_at(n), n)


def build(nc, x, itok, fside, cond_w, gate_w, expert_bias, ffn_w, out):
    x_rows = x.rearrange("b c t -> (b c) t")
    h_rows = nc.dram_tensor("h_rows", [N + P, H + E], F32).ap()

    with ExitStack() as ctx:
        def sb(name, shape, dt=F32):
            return ctx.enter_context(nc.sbuf_tensor(name, shape, dt))

        def ps(name):
            return ctx.enter_context(nc.psum_tensor(name, [P, 512], F32))

        def sem(name):
            return ctx.enter_context(nc.semaphore(name))

        ident = sb("ident", [P, P])
        before = sb("before", [P, P])
        ones = sb("ones", [P, P])
        key16 = sb("key16", [P, E])
        iota_lane = sb("iota_lane", [P, P])
        iota_tile = sb("iota_tile", [P, NRP])
        iota_full = sb("iota_full", [P, NT])
        token1 = sb("token1", [P, NT])
        pad_row = sb("pad_row", [P, 1])
        part_no = sb("part_no", [P, 1])
        itok_row = sb("itok_row", [1, B], I32)
        itok8 = sb("itok8", [NS, B], I32)
        subj1h = sb("subj1h", [NS, B])
        fside2 = sb("fside2", [NS, 2 * C])
        bias_tok = sb("bias_tok", [P, NT])
        gate_sb = sb("gate_sb", [P, HK * E])
        ebias = sb("ebias", [P, E])
        raw_w = sb("raw_w", [P, 2 * EW])
        split_w = sb("split_w", [P, SPLITS * 2 * EW], F32R)
        cond_sb = sb("cond_sb", [P, NS * C])
        x_ring = sb("x_ring", [P, RING, H])
        cw_ring = sb("cw_ring", [P, RING, P])
        tok_ring = sb("tok_ring", [P, RING, H + E])
        aT = sb("aT", [P, 2, H])
        xT_hi = sb("xT_hi", [P, 2, H], F32R)
        xT_lo = sb("xT_lo", [P, 2, H], F32R)
        silu, hid = aT[:, :, 0:I], aT[:, :, I:2 * I]
        hidT_hi = sb("hidT_hi", [P, 2, I], F32R)
        hidT_lo = sb("hidT_lo", [P, 2, I], F32R)
        y_ring = sb("y_ring", [P, RING, H])
        zeros = y_ring[:].rearrange("p r h -> p (r h)")[:, 0:H + E]
        gidx_s = [sb(f"gidx{s}", [P, 1], U32) for s in range(RING)]
        sidx_s = [sb(f"sidx{s}", [P, 1], U32) for s in range(RING)]
        scores = sb("scores", [P, NT * E])
        passing = [raw_w[:, EW + k * NT * E:EW + (k + 1) * NT * E] for k in range(TOPK + 2)]
        assert (TOPK + 2) * NT * E <= EW
        biased, t0, chosen = passing[0], passing[1], passing[2:]
        t1 = sb("t1", [P, NT * E])
        mask = sb("mask", [P, NT * E])
        group_tmp = sb("group_tmp", [P, 6, BC * NG])
        small = [group_tmp[:, k, :] for k in range(6)]
        red = sb("red", [P, NT])
        red2 = sb("red2", [P, NT])
        weights_te = sb("weights_te", [P, NT, E])
        slot_f = sb("slot_f", [P, NT, TOPK])
        slot_i = sb("slot_i", [P, NT * TOPK], I32)
        part_i = sb("part_i", [P, NT * TOPK], I32)
        slot_tile = sb("slot_tile", [P, NT, TOPK])
        slot_lane = sb("slot_lane", [P, NT, TOPK])
        e0 = sb("e0", [P, E])
        e1 = sb("e1", [P, E])
        tiles_e = sb("tiles_e", [P, E])
        size_key = sb("size_key", [P, E])
        rank2 = sb("rank2", [P, E])
        used = sb("used", [P, E])
        n_used = sb("n_used", [P, 1])
        big = sb("big", [P, E])
        turn_e = sb("turn_e", [P, E])
        col_tmp = sb("col_tmp", [E, E])
        used_col, start_col, end_col, turn_col = [sb(f"expert_col{k}", [E, 1]) for k in range(4)]
        begun = sb("begun", [E, NR])
        running = sb("running", [E, NR])
        takes = sb("takes", [E, E + SPLITS + 1])
        n_tiles = sb("n_tiles", [1, 1])
        turn_f = sb("turn_f", [1, NR + 1])
        prep_f = sb("prep_f", [1, NR])
        prep_t = sb("prep_t", [1, NR])
        order = sb("order", [1, E + SPLITS + 1], I32)
        eid = sb("eid", [1, NR], I32)
        turn_i = sb("turn_i", [1, NR], I32)
        woff = sb("woff", [1, NR], I32)
        need = sb("need", [1, NR], I32)
        live = sb("live", [1, E + 1], I32)
        prep_odd = sb("prep_odd", [1, NR], I32)
        prep_third = sb("prep_third", [1, NR], I32)
        opens = sb("opens", [1, NR], I32)
        prep = sb("prep", [1, NR], I32)
        lane1h = sb("lane1h", [P, 2, TOPK, P], F32R)
        entry = sb("entry", [P, 2, TOPK, NRP], F32R)
        idx_all = sb("idx_all", [P, NR], U32)
        pad_tmp = sb("pad_tmp", [P, NR])

        psT = [ps(f"psT{i}") for i in range(2)]
        psGU = [ps(f"psGU{i}") for i in range(2)]
        psY = [ps(f"psY{i}") for i in range(2)]
        psH = ps("psH")
        psM = ps("psM")

        consts = sem("consts")
        pool_step = sem("pool_step")
        small_loaded = sem("small_loaded")
        raw_loaded = sem("raw_loaded")
        shared_loaded = sem("shared_loaded")
        high_ready = sem("high_ready")
        low_a_done = sem("low_a_done")
        low_b_done = sem("low_b_done")
        x_loaded = [sem(f"x_loaded{s}") for s in range(RING)]
        x_in = [sem(f"x_in{s}") for s in range(RING)]
        cond_w_ready = sem("cond_w_ready")
        weights_ready = sem("weights_ready")
        weights_stored = sem("weights_stored")
        xhi_ready = sem("xhi_ready")
        hidhi_ready = sem("hidhi_ready")
        subj_ready = sem("subj_ready")
        bias_ps = sem("bias_ps")
        bias_ready = sem("bias_ready")
        cond_done = sem("cond_done")
        h_ready = sem("h_ready")
        h_stored = [sem(f"h_stored{s}") for s in range(RING)]
        pads_stored = sem("pads_stored")
        a_xposed = sem("a_xposed")
        a_xT_ready = sem("a_xT_ready")
        logits_done = sem("logits_done")
        scored = sem("scored")
        dve = sem("dve")
        mask_ready = sem("mask_ready")
        prefix_done = sem("prefix_done")
        order_ready = sem("order_ready")
        expert_tab = sem("expert_tab")
        turns_ready = sem("turns_ready")
        turns_summed = sem("turns_summed")
        entry_ready = sem("entry_ready")
        table_done = sem("table_done")
        slots_ready = sem("slots_ready")
        h_loaded = [sem(f"h_loaded{s}") for s in range(RING)]
        gathered = [sem(f"gathered{s}") for s in range(RING)]
        out_stored = [sem(f"out_stored{s}") for s in range(RING)]
        scattered = [sem(f"scattered{s}") for s in range(RING)]
        idx_copied = sem("idx_copied")
        pool_clear = sem("pool_clear")
        sp_clear = sem("sp_clear")
        xposed = sem("xposed")
        xT_ready = sem("xT_ready")
        gu_done = sem("gu_done")
        silu_ready = sem("silu_ready")
        hid_ready = sem("hid_ready")
        hid_xposed = sem("hid_xposed")
        hidT_ready = sem("hidT_ready")
        down_done = sem("down_done")
        y_ready = sem("y_ready")

        SMALL = 8 * 16

        COND = (0, RING, NT // RING - 1, 2)
        SHARED = (0, RING, NT // RING - 2, RING)
        TURNS = (NR - AHEAD - RING) // RING
        ROUTED = (NT, NR - AHEAD - RING * TURNS, TURNS, AHEAD)
        LAST = NT + NR - 1
        FIRST_LOADS = [0, 2, NT - RING]
        assert FIRST_LOADS[2] >= NT - SHARED[3] and (E - len(FIRST_LOADS)) % 2

        def split_slot(odd, third, start=0, size=EW):
            return (raw_w[:, bass.ds(odd * EW + start, size)], split_w[:, bass.ds(third * (2 * EW) + start, size)],
                    split_w[:, bass.ds(third * (2 * EW) + (EW + start), size)])

        def rows(t, ap):
            return ap[bass.ds(t.done() * P, P), 0:H]

        block = ctx.enter_context(nc.Block())

        @block.sync
        def _(sp):
            sp.dma_start(itok_row[:], itok.unsqueeze(0)).then_inc(small_loaded, 16)
            sp.dma_start(itok8[:], itok.partition_broadcast(NS)).then_inc(small_loaded, 16)
            for half in range(2):
                sp.dma_start(fside2[:, half * C:(half + 1) * C], fside).then_inc(small_loaded, 16)
                sp.dma_start(cond_sb[half * C:(half + 1) * C, :].rearrange("c (n d) -> c n d", d=C),
                             cond_w.rearrange("n c d -> c n d")).then_inc(small_loaded, 16)
            sp.dma_start(gate_sb[:], gate_w).then_inc(small_loaded, 16)
            sp.dma_start(ebias[:], expert_bias.partition_broadcast(P)).then_inc(small_loaded, 16)

            def load_x(t, n):
                if n is None or n >= RING:
                    sp.wait_ge(cond_done, t.done(1 - RING))
                sp.dma_start(x_ring[:, t.slot, :], rows(t, x_rows)).then_inc(x_in[t.slot], 16)

            for n in range(RING):
                load_x(tile_at(n), n)

            def cond_step(t, n):
                if n is None or n + RING < NT:
                    load_x(t + RING, None if n is None else n + RING)
                elif n + RING == NT:
                    sp.dma_start(raw_w[:, 0:EW], ffn_w[E]).then_inc(shared_loaded, 16)
                sp.wait_ge(h_ready, t.done(1))
                sp.dma_start(rows(t, h_rows), tok_ring[:, t.slot, 0:H]).then_inc(h_stored[t.slot], 16)

            run_tiles(sp, 0, RING, NT // RING - 2, RING, cond_step)

            for s in range(RING):
                sp.wait_ge(h_stored[s], 16 * (NT // RING))

            def load_h(t):
                sp.dma_start(tok_ring[:, t.slot, 0:H], rows(t, h_rows)).then_inc(h_loaded[t.slot], 16)

            def load_residual(t):
                sp.dma_start(x_ring[:, t.slot, :], rows(t, x_rows)).then_inc(x_loaded[t.slot], 16)

            sp.wait_ge(cond_done, NT)
            for n in range(RING):
                load_residual(tile_at(n))
            sp.wait_ge(a_xposed, NT)
            for n in range(RING - 1):
                load_h(tile_at(n))

            def load_raw(turn, odd):
                expert = sp.value_load(order[0:1, bass.ds(turn, 1)], min_val=0, max_val=E - 1)
                sp.dma_start(raw_w[:, odd * EW:(odd + 1) * EW],
                             ffn_w[bass.ds(expert, 1), :, :].rearrange("o p w -> (o p) w")
                             ).then_inc(raw_loaded, 16)

            sp.wait_ge(order_ready, 1)

            def shared_step(t, n):
                if n in FIRST_LOADS:
                    turn = 1 + FIRST_LOADS.index(n)
                    if turn > 1:
                        sp.wait_ge(raw_loaded, 16 * (turn - 1))
                        sp.wait_ge(low_a_done, turn - 1)
                        sp.wait_ge(low_b_done, turn - 1)
                    load_raw(turn, turn % 2)
                if n is None or n + RING - 1 < NT:
                    if n is None or n > 0:
                        sp.wait_ge(xposed, t.done())
                    load_h(t + (RING - 1))
                sp.wait_ge(y_ready, t.done(1))
                sp.dma_start(rows(t, out), y_ring[:, t.slot, :]).then_inc(out_stored[t.slot], 16)
                if n is None or n + RING < NT:
                    load_residual(t + RING)

            run_tiles(sp, *SHARED, shared_step)

            sp.wait_ge(expert_tab, 1)
            def turn_step(turn, odd):
                with sp.If(sp.value_load(live[0:1, bass.ds(turn, 1)], min_val=0, max_val=1)):
                    sp.wait_ge(raw_loaded, (turn + -1) * 16)
                    sp.sem_inc(sp_clear, 1)
                    sp.wait_ge(low_a_done, turn + -1)
                    sp.sem_inc(sp_clear, 1)
                    sp.wait_ge(low_b_done, turn + -1)
                    sp.sem_inc(sp_clear, 1)
                    load_raw(turn, odd)

            with sp.Fori(0, (E - len(FIRST_LOADS)) // 2) as pair:
                for j in range(2):
                    turn_step(pair * 2 + (len(FIRST_LOADS) + 1 + j), j)
            turn_step(E, 0)

        @block.gpsimd
        def _(pool):
            count = [0]

            def link(ins):
                count[0] += 1
                ins.then_inc(pool_step, 1)
                pool.wait_ge(pool_step, count[0])

            link(pool.memset(cw_ring[:], 0.0))
            link(pool.memset(zeros, 0.0))
            link(pool.memset(ident[:], 0.0))
            link(pool.memset(ones[:], 1.0))
            link(pool.affine_select(out=ident[:], in_=ident[:], compare_op=ALU.not_equal, fill=1.0,
                                    base=0, pattern=[[-1, P]], channel_multiplier=1))
            link(pool.affine_select(out=before[:], in_=ones[:], compare_op=ALU.is_gt, fill=0.0,
                                    base=0, pattern=[[1, P]], channel_multiplier=-1))

            def iota(t, step, base, per_partition):
                link(pool.iota(t[:], [[step, t.shape[1]]], base=base, channel_multiplier=per_partition,
                               allow_small_or_imprecise_dtypes=True))

            iota(key16, -1, E, 0)
            iota(iota_lane, 1, 0, 0)
            iota(iota_tile, 1, 0, 0)
            iota(iota_full, P, 0, 0)
            iota(token1, P, 1, 1)
            iota(pad_row, 0, N + 1, 1)
            iota(part_no, 0, 0, 1)
            pool.sem_inc(consts, 1)
            pool.dma_start(h_rows[N:N + P, :], zeros).then_inc(pads_stored, 16)
            pool.dma_start(out[N:N + P, :], zeros[:, 0:H]).then_inc(pads_stored, 16)

            pool.wait_ge(small_loaded, SMALL)

            def cond_step(t, n):
                for half in range(2):
                    subject = pool.value_load(itok_row[0:1, bass.ds(t.done() * 2 + half, 1)],
                                              min_val=0, max_val=NS - 1)
                    if half == 0 and (n is None or n >= RING):
                        pool.wait_ge(cond_done, t.done(1 - RING))
                        pool.sem_inc(pool_clear, 1)
                    a, b = half * C, half * C + C
                    pool.tensor_copy(cw_ring[a:b, t.slot, a:b],
                                     cond_sb[a:b, bass.ds(subject * C, C)]).then_inc(cond_w_ready, 1)

            run_tiles(pool, COND[0], COND[1], COND[2], 0, cond_step)

            def split_low(odd, third, turn):
                pool.wait_ge(high_ready, turn * 2 + 2)
                for start, size, done in ((0, UP, low_a_done), (UP, EW - UP, low_b_done)):
                    raw, high, low = split_slot(odd, third, start, size)
                    pool.tensor_tensor(low, raw, high.bitcast(F32), ALU.subtract).then_inc(done, 1)

            pool.wait_ge(cond_w_ready, 2 * NT)
            split_low(0, 0, 0)
            pool.wait_ge(weights_ready, NB)
            pool.dma_start(h_rows[0:N, H:H + E].rearrange("(c p) e -> p c e", p=P), weights_te[:]
                           ).then_inc(weights_stored, 16)

            split_low(1, 1, 1)
            split_low(0, 2, 2)

            pool.wait_ge(weights_stored, 16)
            pool.wait_ge(expert_tab, 1)
            pool.wait_ge(slots_ready, 1)
            pool.wait_ge(pads_stored, 32)
            for s in range(RING):
                pool.wait_ge(h_stored[s], 16 * (NT // RING))

            def copy_idx(dst, t, nth):
                pool.tensor_copy(dst[:], idx_all[:, bass.ds(t.done(-NT), 1)]).then_inc(idx_copied, 1)
                pool.wait_ge(idx_copied, nth)

            def gather(t, nth):
                copy_idx(gidx_s[t.slot], t, nth)
                pool.sem_inc(pool_clear, 1)
                pool.indirect_dma_start(tok_ring[:, t.slot, :], None, h_rows[:, :],
                                        bass.IndirectOffsetOnAxis(gidx_s[t.slot][:], 0)
                                        ).then_inc(gathered[t.slot], 16)

            def scatter(t, n, nth):
                copy_idx(sidx_s[t.slot], t, nth)
                pool.wait_ge(y_ready, t.done(1))
                pool.sem_inc(pool_clear, 1)
                if n != NT:
                    with pool.If(pool.value_load(opens[0:1, bass.ds(t.done(-NT), 1)], min_val=0, max_val=1)):
                        for s in range(RING):
                            if n is None or n >= NT + RING or s < t.slot:
                                pool.wait_ge(scattered[s], (t.rnd - NT // RING + (1 if s < t.slot else 0)) * 16)
                        pool.sem_inc(pool_clear, 1)
                pool.indirect_dma_start(out[:, :], bass.IndirectOffsetOnAxis(sidx_s[t.slot][:], 0),
                                        y_ring[:, t.slot, :], None, compute_op=ALU.add
                                        ).then_inc(scattered[t.slot], 16)

            pool.wait_ge(xposed, NT)
            for n in range(AHEAD):
                gather(tile_at(NT + n), n + 1)
            for s in range(RING):
                pool.wait_ge(out_stored[s], 16 * (NT // RING))

            def routed_step(t, n):
                r = t.done(-NT)
                if n is None or n + AHEAD <= LAST:
                    if n != NT:
                        pool.wait_ge(hid_ready, t.done(AHEAD - RING + 1))
                    gather(t + AHEAD, r * 2 + AHEAD + (1 if n == NT else 0))
                    nth = r * 2 + AHEAD + 1
                else:
                    nth = NR + r
                if n != NT:
                    scatter(t + -1, None if n is None else n - 1, nth)
                    next_weights(r + -1)

            def next_weights(r):
                turn = pool.value_load(prep[0:1, bass.ds(r, 1)], min_val=0, max_val=E)
                with pool.If(turn):
                    odd = pool.value_load(prep_odd[0:1, bass.ds(r, 1)], min_val=0, max_val=1)
                    third = pool.value_load(prep_third[0:1, bass.ds(r, 1)], min_val=0, max_val=SPLITS - 1)
                    raw, high, low = split_slot(odd, third, 0, UP)
                    pool.wait_ge(high_ready, turn * 2 + 2)
                    pool.sem_inc(pool_clear, 1)
                    pool.tensor_tensor(low, raw, high.bitcast(F32), ALU.subtract).then_inc(low_a_done, 1)

            run_tiles(pool, *ROUTED, routed_step)
            scatter(tile_at(LAST), LAST, 2 * NR)
            for s in range(RING):
                pool.wait_ge(scattered[s], 16 * ((NR + RING - 1 - s) // RING))

        @block.scalar
        def _(act):
            act.wait_ge(bias_ready, 2)

            def cond_step(t, n):
                if n is None or n < NT:
                    act.wait_ge(cond_done, t.done(1))
                    if n is None or n >= RING:
                        act.wait_ge(h_stored[t.slot], t.rnd * 16)
                        act.wait_ge(a_xposed, t.done(1 - RING))
                    act.activation(tok_ring[:, t.slot, 0:H], psY[t.slot % 2][:], ACT.Identity,
                                   bias=bias_tok[:, bass.ds(t.done(), 1)]).then_inc(h_ready, 1)
                if n is None or 1 <= n <= NT:
                    act.wait_ge(a_xposed, t.done())
                    if n is None or n >= 3:
                        act.wait_ge(logits_done, t.done(-2))
                    act.activation(aT[:, (t.slot + 1) % 2, :], psT[(t.slot + 1) % 2][:], ACT.Copy
                                   ).then_inc(a_xT_ready, 1)
                if n is None or n >= 2:
                    act.wait_ge(logits_done, t.done(-1))
                    act.activation(scores[:, bass.ds(t.done(-2) * E, E)], psGU[t.slot % 2][:, 0:E],
                                   ACT.Sigmoid).then_inc(scored, 1)

            run_tiles(act, *COND, cond_step)

            def copy_xT(t, n):
                act.wait_ge(xposed, t.done(1))
                if n is None or n >= 2:
                    act.wait_ge(gu_done, t.done(-1))
                act.activation(xT_hi[:, t.slot % 2, :], psT[t.slot % 2][:], ACT.Copy).then_inc(xhi_ready, 1)

            def copy_hidT(t, n):
                act.wait_ge(hid_xposed, t.done(1))
                if n is None or n >= 2:
                    act.wait_ge(down_done, t.done(-1))
                act.activation(hidT_hi[:, t.slot % 2, :], psH[:, 0:I], ACT.Copy).then_inc(hidhi_ready, 1)

            def split_high(odd, third):
                raw, high, low = split_slot(odd, third)
                act.activation(high, raw, ACT.Copy).then_inc(high_ready, 2)

            def next_weights(t, first_part):
                turn = act.value_load(prep[0:1, bass.ds(t.done(-NT), 1)], min_val=0, max_val=E)
                with act.If(turn):
                    odd = act.value_load(prep_odd[0:1, bass.ds(t.done(-NT), 1)], min_val=0, max_val=1)
                    third = act.value_load(prep_third[0:1, bass.ds(t.done(-NT), 1)], min_val=0, max_val=SPLITS - 1)
                    raw, high, low = split_slot(odd, third, 0 if first_part else UP,
                                                UP if first_part else EW - UP)
                    if first_part:
                        act.wait_ge(raw_loaded, turn * 16)
                        act.wait_ge(gu_done, t.done())
                    else:
                        act.wait_ge(down_done, t.done())
                    act.activation(high, raw, ACT.Copy).then_inc(high_ready, 1)

            def ffn(run, last, routed):
                first = run[0]

                def step(t, n):
                    if n != first:
                        copy_hidT(t + -1, None if n is None else n - 1)
                    if n is None or n < last:
                        copy_xT(t + 1, None if n is None else n + 1)
                    if routed and n != first:
                        next_weights(t + -1, False)
                    act.wait_ge(gu_done, t.done(1))
                    if n is None or n >= 2:
                        act.wait_ge(hid_ready, t.done(-1))
                    act.activation(silu[:, t.slot % 2, :], psGU[t.slot % 2][:, 0:I], ACT.Silu
                                   ).then_inc(silu_ready, 1)
                    if routed:
                        next_weights(t, True)
                    elif n == RING - 1:
                        act.wait_ge(raw_loaded, 16)
                        split_high(1, 1)
                    elif n == NT - RING:
                        act.wait_ge(raw_loaded, 32)
                        split_high(0, 2)

                copy_xT(tile_at(first), first)
                run_tiles(act, *run, step)
                copy_hidT(tile_at(last), last)

            act.wait_ge(shared_loaded, 16)
            split_high(0, 0)
            ffn(SHARED, NT - 1, False)
            act.wait_ge(expert_tab, 1)
            ffn(ROUTED, LAST, True)

        @block.tensor
        def _(pe):
            pe.wait_ge(consts, 1)
            pe.wait_ge(small_loaded, SMALL)
            pe.wait_ge(subj_ready, 1)
            subj = subj1h[:, :].rearrange("n (c two) -> n two c", two=2)
            for half in range(2):
                mm = pe.matmul(psH[:, half * NT:(half + 1) * NT], fside2[:], subj[:, half, :],
                               start=True, stop=True)
            mm.then_inc(bias_ps, 1)

            def transposes(dst, src, parts):
                for k in range(parts):
                    mm = pe.transpose(dst[:, k * P:(k + 1) * P], src[:, k * P:(k + 1) * P], ident[:])
                return mm

            def cond_step(t, n):
                if n is None or n < NT:
                    pe.wait_ge(x_in[t.slot], (t.rnd + 1) * 16)
                    pe.wait_ge(cond_w_ready, t.done(1) * 2)
                    if n is None or n >= 2:
                        pe.wait_ge(h_ready, t.done(-1))
                    pe.matmul(psY[t.slot % 2][:], cw_ring[:, t.slot, :], x_ring[:, t.slot, :],
                              start=True, stop=True).then_inc(cond_done, 1)
                if n is None or 1 <= n <= NT:
                    u = t + -1
                    pe.wait_ge(h_ready, t.done())
                    if n is None or n >= 3:
                        pe.wait_ge(a_xT_ready, t.done(-2))
                    transposes(psT[u.slot % 2], tok_ring[:, u.slot, 0:H], HK).then_inc(a_xposed, 1)
                if n is None or n >= 2:
                    pe.wait_ge(a_xT_ready, t.done(-1))
                    if n is None or n >= 4:
                        pe.wait_ge(scored, t.done(-3))
                    for k in range(HK):
                        mm = pe.matmul(psGU[t.slot % 2][:, 0:E], aT[:, t.slot % 2, k * P:(k + 1) * P],
                                       gate_sb[:, k * E:(k + 1) * E], start=(k == 0), stop=(k == HK - 1))
                    mm.then_inc(logits_done, 1)

            run_tiles(pe, *COND, cond_step)
            pe.wait_ge(scored, NT)
            pe.wait_ge(mask_ready, NB)
            pe.matmul(psH[:], before[:], mask[:], start=True, stop=True)
            pe.matmul(psM[:], ones[:], mask[:], start=True, stop=True).then_inc(prefix_done, 1)
            pe.wait_ge(turns_ready, 1)
            for lhs, table, at in ((ones, begun, 0), (part_no, running, NR), (part_no, takes, 2 * NR)):
                mm = pe.matmul(psM[0:1, at:at + table.shape[1]], lhs[0:E, 0:1], table[:], start=True, stop=True)
            mm.then_inc(turns_summed, 1)
            pe.wait_ge(low_a_done, 1)
            pe.wait_ge(low_b_done, 1)

            def xpose(t, n, routed):
                if routed:
                    pe.wait_ge(gathered[t.slot], (t.rnd - (NT // RING - 1)) * 16)
                else:
                    pe.wait_ge(h_loaded[t.slot], (t.rnd + 1) * 16)
                if n is None or n >= 2:
                    pe.wait_ge(xT_ready, t.done(-1))
                transposes(psT[t.slot % 2], tok_ring[:, t.slot, 0:H], HK).then_inc(xposed, 1)

            def xpose_hid(t, n):
                pe.wait_ge(hid_ready, t.done(1))
                if n is None or n >= 1:
                    pe.wait_ge(hidT_ready, t.done())
                transposes(psH, hid[:, t.slot % 2, :], IK).then_inc(hid_xposed, 1)

            def weights(t, routed):
                if not routed:
                    return lambda col: split_w[:, col:col + H]
                at = pe.value_load(woff[0:1, bass.ds(t.done(-NT), 1)], min_val=0, max_val=(SPLITS - 1) * 2 * EW)
                return lambda col: split_w[:, bass.ds(at + col, H)]

            def split_product(dst, high, low, slot, parts, w, col):
                for k in range(parts):
                    c = slice(k * P, (k + 1) * P)
                    for a, at in ((high, 0), (high, EW), (low, 0)):
                        mm = pe.matmul(dst, a[:, slot, c], w(at + col + k * H), start=(k == 0 and a is high and at == 0),
                                       stop=(k == parts - 1 and a is low))
                return mm

            def gate_up(t, n, w, needed):
                if needed is not None:
                    pe.wait_ge(low_a_done, needed)
                    pe.wait_ge(low_b_done, needed)
                pe.wait_ge(xT_ready, t.done(1))
                if n is None or n >= 2:
                    pe.wait_ge(hid_ready, t.done(-1))
                split_product(psGU[t.slot % 2][:], xT_hi, xT_lo, t.slot % 2, HK, w, 0).then_inc(gu_done, 1)

            def down(t, n, w):
                pe.wait_ge(hidT_ready, t.done(1))
                if n is None or n >= 2:
                    pe.wait_ge(y_ready, t.done(-1))
                split_product(psY[t.slot % 2][:], hidT_hi, hidT_lo, t.slot % 2, IK, w, UP).then_inc(down_done, 1)

            def fill_slots(t, n):
                pe.wait_ge(entry_ready, t.done(1))
                for k in range(TOPK):
                    mm = pe.matmul(psM[:, 0:NRP], lane1h[:, t.slot % 2, k, :], entry[:, t.slot % 2, k, :],
                                   start=(n == 0 and k == 0), stop=(n == NT - 1 and k == TOPK - 1),
                                   skip_group_check=True)
                mm.then_inc(table_done, 1)

            def ffn(run, last, routed):
                first = run[0]

                def step(t, n):
                    prev = None if n is None else n - 1
                    w = weights(t, routed)
                    needed = None
                    if routed:
                        needed = pe.value_load(need[0:1, bass.ds(t.done(-NT), 1)], min_val=1, max_val=E + 1)
                    w_prev = weights(t + -1, routed) if n != first else None
                    if n is None or n < last:
                        xpose(t + 1, None if n is None else n + 1, routed)
                    if n != first:
                        xpose_hid(t + -1, prev)
                    gate_up(t, n, w, needed)
                    if n != first:
                        down(t + -1, prev, w_prev)
                        if not routed:
                            fill_slots(t + -1, prev)

                xpose(tile_at(first), first, routed)
                run_tiles(pe, *run, step)
                w = weights(tile_at(last), routed)
                xpose_hid(tile_at(last), last)
                if not routed:
                    fill_slots(tile_at(last), last)
                down(tile_at(last), last, w)

            ffn(SHARED, NT - 1, False)
            pe.wait_ge(expert_tab, 1)
            ffn(ROUTED, LAST, True)

        @block.vector
        def _(v):
            count, before_loop = [0], [0]

            def link(ins):
                count[0] += 1
                ins.then_inc(dve, 1)
                v.wait_ge(dve, before_loop[0] + count[0])

            def tt(o, a, b, op):
                link(v.tensor_tensor(o, a, b, op))

            v.wait_ge(consts, 1)
            v.wait_ge(small_loaded, SMALL)
            v.tensor_scalar(subj1h[:], itok8[:], part_no[0:NS, 0:1], None, ALU.is_equal).then_inc(subj_ready, 1)
            v.wait_ge(bias_ps, 1)
            for half in range(2):
                a, b = half * C, half * C + C
                v.tensor_copy(bias_tok[a:b, :], psH[a:b, half * NT:(half + 1) * NT]).then_inc(bias_ready, 1)

            def per_chunk(ap, n):
                return ap.rearrange("p (c n) -> p c n", n=n)

            def spread(ap, n):
                return ap.unsqueeze(2).to_broadcast([P, ap.shape[1], n])

            def over_chunks(ap, chunks):
                return ap.unsqueeze(1).to_broadcast([P, chunks, ap.shape[1]])

            def pick(onehot, values, n, keys, again):
                val, one, tmp = per_chunk(values, n), per_chunk(onehot, n), per_chunk(t1[:, 0:BC * n], n)
                link(v.tensor_reduce(red[:, 0:BC], val, AX.X, ALU.max))
                tt(tmp, val, spread(red[:, 0:BC], n), ALU.is_equal)
                tt(tmp, tmp, over_chunks(keys, BC), ALU.mult)
                link(v.tensor_reduce(red2[:, 0:BC], tmp, AX.X, ALU.max))
                tt(one, tmp, spread(red2[:, 0:BC], n), ALU.is_equal)
                if again:
                    link(v.scalar_tensor_tensor(out=values, in0=onehot, scalar=-BIG, in1=values,
                                                op0=ALU.mult, op1=ALU.add))

            ROUTE_LINKS = 54
            values, others = biased[:, 0:BC * E], t0[:, 0:BC * E]
            start_links = count[0]
            with v.Fori(0, NB) as b:
                before_loop[0] = b * ROUTE_LINKS

                def of_batch(table):
                    return table[:, bass.ds(b * (BC * E), BC * E)]

                v.wait_ge(scored, b * BC + BC)
                tt(per_chunk(values, E), per_chunk(of_batch(scores), E), over_chunks(ebias[:], BC), ALU.add)
                four = values.rearrange("p (g j) -> p j g", j=GS)
                hi1, lo1, hi2, lo2, s4, s5 = small
                tt(hi1, four[:, 0, :], four[:, 1, :], ALU.max)
                tt(lo1, four[:, 0, :], four[:, 1, :], ALU.min)
                tt(hi2, four[:, 2, :], four[:, 3, :], ALU.max)
                tt(lo2, four[:, 2, :], four[:, 3, :], ALU.min)
                tt(s4, hi1, hi2, ALU.max)
                tt(s5, hi1, hi2, ALU.min)
                tt(lo1, lo1, lo2, ALU.max)
                tt(s5, s5, lo1, ALU.max)
                tt(s4, s4, s5, ALU.add)
                pick(hi1, s4, NG, key16[:, E - NG:E], True)
                pick(hi2, s4, NG, key16[:, E - NG:E], False)
                tt(hi1, hi1, hi2, ALU.add)
                link(v.tensor_scalar(hi1, hi1, -1.0, BIG, ALU.add, ALU.mult))
                by_group = values.rearrange("p (g j) -> p g j", j=GS)
                tt(by_group, by_group, spread(hi1, GS), ALU.add)
                for k in range(TOPK):
                    pick(of_batch(chosen[k]), values, E, key16[:], k < TOPK - 1)
                tt(of_batch(mask), of_batch(chosen[0]), of_batch(chosen[1]), ALU.add)
                tt(others, of_batch(chosen[2]), of_batch(chosen[3]), ALU.add)
                v.tensor_tensor(of_batch(mask), of_batch(mask), others, ALU.add).then_inc(mask_ready, 1)
                v.wait_ge(mask_ready, b + 1)

                total_w = red[:, 0:BC]
                tt(values, of_batch(mask), of_batch(scores), ALU.mult)
                link(v.tensor_reduce(total_w, per_chunk(values, E), AX.X, ALU.add))
                link(v.tensor_scalar(total_w, total_w, 1e-20, None, ALU.add))
                link(v.reciprocal(total_w, total_w))
                tt(per_chunk(values, E), per_chunk(values, E), spread(total_w, E), ALU.mult)
                v.tensor_scalar(weights_te[:, bass.ds(b * BC, BC), :].rearrange("p c e -> p (c e)"), values,
                                SCALING, None, ALU.mult).then_inc(weights_ready, 1)
                v.wait_ge(weights_ready, b + 1)
            assert count[0] - start_links == ROUTE_LINKS, count[0] - start_links
            before_loop[0] = 0
            count[0] += (NB - 1) * ROUTE_LINKS

            v.wait_ge(prefix_done, 1)
            link(v.tensor_copy(t0[:], psM[:]))
            src, dst = t0, t1
            d = 1
            while d < NT:
                v.tensor_copy(dst[:, 0:d * E], src[:, 0:d * E])
                tt(dst[:, d * E:], src[:, d * E:], src[:, 0:(NT - d) * E], ALU.add)
                src, dst = dst, src
                d *= 2
            total = src[:, (NT - 1) * E:NT * E]
            steps = biased[:, :].rearrange("p (e j) -> p e j", j=NT)
            tt(steps, spread(total, NT), iota_full[:].unsqueeze(1).to_broadcast([P, E, NT]), ALU.is_gt)
            link(v.tensor_reduce(tiles_e[:], steps, AX.X, ALU.add))
            link(v.scalar_tensor_tensor(out=size_key[:], in0=total, scalar=float(E), in1=key16[:],
                                        op0=ALU.mult, op1=ALU.add))
            pairs = biased[:, 0:E * E].rearrange("p (e j) -> p e j", j=E)

            def of_e(ap):
                return ap.unsqueeze(2).to_broadcast([P, E, E])

            def of_j(ap):
                return ap.unsqueeze(1).to_broadcast([P, E, E])

            tt(pairs, of_j(size_key[:]), of_e(size_key[:]), ALU.is_gt)
            link(v.tensor_reduce(rank2[:], pairs, AX.X, ALU.add))
            link(v.tensor_scalar(rank2[:], rank2[:], 2.0, None, ALU.mult))
            link(v.tensor_scalar(used[:], tiles_e[:], 0.0, None, ALU.is_gt))
            link(v.tensor_reduce(n_used[:], used[:], AX.X, ALU.add))
            link(v.tensor_scalar(big[:], rank2[:], n_used[:, 0:1], None, ALU.is_lt))
            link(v.tensor_scalar(e0[:], rank2[:], -1.0, n_used[:, 0:1], ALU.mult, ALU.add))
            link(v.tensor_scalar(e0[:], e0[:], n_used[:, 0:1], None, ALU.add))
            link(v.tensor_scalar(e1[:], rank2[:], 1.0, None, ALU.add))
            tt(e1[:], e1[:], e0[:], ALU.subtract)
            tt(e1[:], e1[:], big[:], ALU.mult)
            tt(e0[:], e0[:], e1[:], ALU.add)
            tt(turn_e[:], e0[:], used[:], ALU.mult)
            starts, ends = e0, e1
            tt(pairs, of_j(turn_e[:]), of_e(turn_e[:]), ALU.is_lt)
            tt(pairs, pairs, of_j(tiles_e[:]), ALU.mult)
            link(v.tensor_reduce(starts[:], pairs, AX.X, ALU.add))
            tt(ends[:], starts[:], tiles_e[:], ALU.add)
            for col, row in ((used_col, used), (start_col, starts), (end_col, ends), (turn_col, turn_e)):
                tt(col_tmp[:], row[0:E, :], ident[0:E, 0:E], ALU.mult)
                link(v.tensor_reduce(col[:], col_tmp[:], AX.X, ALU.add))
            tiles = iota_tile[0:E, 0:NR]
            link(v.tensor_scalar(begun[:], tiles, start_col[:, 0:1], used_col[:, 0:1], ALU.is_ge, ALU.mult))
            link(v.tensor_scalar(running[:], tiles, end_col[:, 0:1], used_col[:, 0:1], ALU.is_ge, ALU.mult))
            tt(running[:], begun[:], running[:], ALU.subtract)
            link(v.tensor_scalar(starts[:], starts[:], float(P), None, ALU.mult))
            link(v.tensor_reduce(n_tiles[:], tiles_e[0:1, :], AX.X, ALU.add))
            link(v.tensor_tensor(dst[:], src[:], psM[:], ALU.subtract))
            v.tensor_scalar(takes[:], iota_tile[0:E, 0:E + SPLITS + 1], turn_col[:, 0:1], None, ALU.is_equal
                            ).then_inc(turns_ready, 1)
            tt(dst[:], dst[:], psH[:], ALU.add)
            tt(per_chunk(dst[:], E), per_chunk(dst[:], E), over_chunks(starts[:], NT), ALU.add)
            for k in range(TOPK):
                tt(src[:], chosen[k][:], dst[:], ALU.mult)
                link(v.tensor_reduce(slot_f[:, :, k], per_chunk(src[:], E), AX.X, ALU.add))
            link(v.tensor_copy(slot_i[:], slot_f[:].rearrange("p c k -> p (c k)")))
            link(v.tensor_scalar(part_i[:], slot_i[:], P.bit_length() - 1, None, ALU.logical_shift_right))
            link(v.tensor_copy(slot_tile[:].rearrange("p c k -> p (c k)"), part_i[:]))
            link(v.tensor_scalar(part_i[:], slot_i[:], P - 1, None, ALU.bitwise_and))
            link(v.tensor_copy(slot_lane[:].rearrange("p c k -> p (c k)"), part_i[:]))
            v.wait_ge(turns_summed, 1)
            link(v.memset(turn_f[:, 0:1], 0.0))
            link(v.tensor_copy(turn_f[:, 1:NR + 1], psM[0:1, 0:NR]))
            link(v.tensor_copy(eid[:], psM[0:1, NR:2 * NR]))
            v.tensor_copy(order[:], psM[0:1, 2 * NR:2 * NR + E + SPLITS + 1]).then_inc(order_ready, 1)
            turn_t = turn_f[:, 1:NR + 1]

            def remainder(o, turn):
                link(v.tensor_scalar(turn_i[:], turn, 86.0, None, ALU.mult))
                link(v.tensor_scalar(turn_i[:], turn_i[:], 8, None, ALU.logical_shift_right))
                link(v.scalar_tensor_tensor(out=o, in0=turn_i[:], scalar=-float(SPLITS), in1=turn,
                                            op0=ALU.mult, op1=ALU.add))

            def turn_tables(n):
                if n == 0:
                    link(v.tensor_scalar(need[:], turn_t, 1.0, None, ALU.add))
                    link(v.tensor_scalar(live[:], iota_tile[0:1, 0:E + 1], n_used[0:1, 0:1], None, ALU.is_le))
                elif n == 1:
                    remainder(woff[:], turn_t)
                    link(v.tensor_scalar(woff[:], woff[:], float(2 * EW), None, ALU.mult))
                elif n == 2:
                    tt(prep_t[:], turn_t, turn_f[:, 0:NR], ALU.not_equal)
                    link(v.tensor_scalar(prep_f[:], iota_tile[0:1, 0:NR], n_tiles[:, 0:1], None, ALU.is_ge))
                    tt(opens[:], prep_t[:], prep_f[:], ALU.max)
                elif n == 3:
                    link(v.tensor_scalar(prep_f[:], turn_t, float(SPLITS - 1), None, ALU.add))
                    tt(prep_t[:], prep_t[:], prep_f[:], ALU.mult)
                    link(v.tensor_scalar(prep_f[:], prep_f[:], n_used[0:1, 0:1], None, ALU.is_le))
                    tt(prep_t[:], prep_t[:], prep_f[:], ALU.mult)
                elif n == 4:
                    link(v.tensor_copy(prep[:], prep_t[:]))
                    remainder(prep_third[:], prep_t[:])
                elif n == 5:
                    v.tensor_scalar(prep_odd[:], prep[:], 1, None, ALU.bitwise_and).then_inc(expert_tab, 1)

            def split_x(t):
                v.wait_ge(xhi_ready, t.done(1))
                v.tensor_tensor(xT_lo[:, t.slot % 2, :], psT[t.slot % 2][:], xT_hi[:, t.slot % 2, :].bitcast(F32),
                                ALU.subtract).then_inc(xT_ready, 1)

            def split_hid(t):
                v.wait_ge(hidhi_ready, t.done(1))
                v.tensor_tensor(hidT_lo[:, t.slot % 2, :], psH[:, 0:I], hidT_hi[:, t.slot % 2, :].bitcast(F32),
                                ALU.subtract).then_inc(hidT_ready, 1)

            def mix(t, n, expert):
                v.wait_ge(silu_ready, t.done(1))
                if n is None or n >= 2:
                    v.wait_ge(hid_xposed, t.done(-1))
                half = t.slot % 2
                gate, up = silu[:, half, :], psGU[half][:, I:2 * I]
                if expert is None:
                    ins = v.tensor_tensor(hid[:, half, :], gate, up, ALU.mult)
                else:
                    ins = v.scalar_tensor_tensor(out=hid[:, half, :], in0=gate,
                                                 scalar=tok_ring[:, t.slot, bass.ds(expert + H, 1)],
                                                 in1=up, op0=ALU.mult, op1=ALU.mult)
                ins.then_inc(hid_ready, 1)

            def finish(t, n, routed):
                v.wait_ge(down_done, t.done(1))
                if routed:
                    if n is None or n >= NT + RING:
                        v.wait_ge(scattered[t.slot], (t.rnd - NT // RING) * 16)
                    else:
                        v.wait_ge(out_stored[t.slot], 16 * (NT // RING))
                    v.tensor_copy(y_ring[:, t.slot, :], psY[t.slot % 2][:]).then_inc(y_ready, 1)
                else:
                    if n is None or n >= RING:
                        v.wait_ge(out_stored[t.slot], t.rnd * 16)
                    elif n < 2:
                        v.wait_ge(pads_stored, 32)
                    v.wait_ge(x_loaded[t.slot], (t.rnd + 1) * 16)
                    v.tensor_tensor(y_ring[:, t.slot, :], psY[t.slot % 2][:], x_ring[:, t.slot, :],
                                    ALU.add).then_inc(y_ready, 1)

            def make_entries(t, n):
                c = t.done()
                if n is None or n >= 2:
                    v.wait_ge(table_done, t.done(-1))
                half = t.slot % 2
                lanes = slot_lane[:, bass.ds(c, 1), :].rearrange("p o k -> p (o k)")
                v.tensor_tensor(lane1h[:, half], iota_lane[:].unsqueeze(1).to_broadcast([P, TOPK, P]),
                                lanes.unsqueeze(2).to_broadcast([P, TOPK, P]), ALU.is_equal)
                for k in range(TOPK):
                    ins = v.tensor_scalar(entry[:, half, k, :], iota_tile[:],
                                          slot_tile[:, bass.ds(c, 1), k:k + 1].rearrange("p o k -> p (o k)"),
                                          token1[:, bass.ds(c, 1)], ALU.is_equal, ALU.mult)
                ins.then_inc(entry_ready, 1)

            def next_weights(r):
                turn = v.value_load(prep[0:1, bass.ds(r, 1)], min_val=0, max_val=E)
                with v.If(turn):
                    odd = v.value_load(prep_odd[0:1, bass.ds(r, 1)], min_val=0, max_val=1)
                    third = v.value_load(prep_third[0:1, bass.ds(r, 1)], min_val=0, max_val=SPLITS - 1)
                    raw, high, low = split_slot(odd, third, UP, EW - UP)
                    v.wait_ge(high_ready, turn * 2 + 2)
                    v.wait_ge(low_b_done, turn)
                    v.tensor_tensor(low, raw, high.bitcast(F32), ALU.subtract).then_inc(low_b_done, 1)

            def fill_idx():
                v.wait_ge(table_done, NT)
                link(v.tensor_scalar(pad_tmp[:], psM[:, 0:NR], 0.0, pad_row[:, 0:1], ALU.is_equal, ALU.mult))
                v.scalar_tensor_tensor(out=idx_all[:], in0=psM[:, 0:NR], scalar=-1.0, in1=pad_tmp[:],
                                       op0=ALU.add, op1=ALU.add).then_inc(slots_ready, 1)

            def ffn(run, last, routed):
                first = run[0]

                def step(t, n):
                    expert = None
                    if routed:
                        expert = v.value_load(eid[0:1, bass.ds(t.done(-NT), 1)], min_val=0, max_val=E - 1)
                    if n != first:
                        split_hid(t + -1)
                    if n is None or n < last:
                        split_x(t + 1)
                    if routed and (n is None or n >= first + 2):
                        next_weights(t.done(-NT - 2))
                    mix(t, n, expert)
                    if n != first:
                        finish(t + -1, None if n is None else n - 1, routed)
                    if not routed:
                        make_entries(t, n)
                        if n is not None and n < first + RING:
                            turn_tables(n - first)

                split_x(tile_at(first))
                run_tiles(v, *run, step)
                split_hid(tile_at(last))
                if not routed:
                    fill_idx()
                finish(tile_at(last), last, routed)

            ffn(SHARED, NT - 1, False)
            v.wait_ge(expert_tab, 1)
            ffn(ROUTED, LAST, True)


def kernel(x, itok_B_0_7, fside_8xS_0, L0_cond_weights, L0_ffn_gate_weight, L0_ffn_expert_bias,
           L0_ffn_gate_proj, L0_ffn_up_proj, L0_ffn_down_proj, L0_ffn_shared_gate, L0_ffn_shared_up,
           L0_ffn_shared_down):
    import numpy as np
    import concourse.bacc as bacc
    from concourse.bass_utils import run_bass_kernel_spmd as run

    def columns(w):
        e, n, k = w.shape
        return w.transpose(0, 2, 1).reshape(e, k // P, P, n).transpose(0, 2, 1, 3)

    gate = np.concatenate([L0_ffn_gate_proj, np.asarray(L0_ffn_shared_gate)[None]])
    up = np.concatenate([L0_ffn_up_proj, np.asarray(L0_ffn_shared_up)[None]])
    down = np.concatenate([L0_ffn_down_proj, np.asarray(L0_ffn_shared_down)[None]])
    ffn_w = np.concatenate([np.concatenate([columns(gate), columns(up)], axis=3).reshape(E + 1, P, UP),
                            columns(down).reshape(E + 1, P, IK * H)], axis=2)
    arrays = {
        "x": np.ascontiguousarray(x),
        "itok": np.ascontiguousarray(itok_B_0_7),
        "fside": np.ascontiguousarray(fside_8xS_0),
        "cond_w": np.ascontiguousarray(L0_cond_weights),
        "gate_w": np.ascontiguousarray(columns(np.asarray(L0_ffn_gate_weight)[None])[0].reshape(P, HK * E)),
        "expert_bias": np.ascontiguousarray(L0_ffn_expert_bias),
        "ffn_w": np.ascontiguousarray(ffn_w),
    }
    nc = bacc.Bacc("TRN2", target_bir_lowering=False, num_devices=1)
    args = [nc.dram_tensor(n, a.shape, mybir.dt.from_np(a.dtype), kind="ExternalInput").ap()
            for n, a in arrays.items()]
    out = nc.dram_tensor("out", [N + P, H], F32, kind="ExternalOutput").ap()
    build(nc, *args, out)
    r = run(nc, [arrays], core_ids=[0])
    return r.results[0]["out"][:N].reshape(B, C, H)
```
